# Optimizing a Trainium2 kernel written in Bass

```python
import numpy as np
import jax
import jax.numpy as jnp

def _softmax(x, axis=-1):
    return jax.nn.softmax(x, axis=axis)

def _gelu(x):
    return jax.nn.gelu(x, approximate=True)

def _silu(x):
    return jax.nn.silu(x)

def _sigmoid(x):
    return jax.nn.sigmoid(x)

def _layernorm(x, axis=-1, eps=1e-05):
    m = jnp.mean(x, axis=axis, keepdims=True)
    v = jnp.var(x, axis=axis, keepdims=True)
    return (x - m) / jnp.sqrt(v + eps)

def _scatter_add(tgt, idx, src, axis=0):
    return tgt.at[idx].add(src)

def _segment_sum(src, seg, n):
    return jax.ops.segment_sum(src, seg, n)
kernel_name = 'mk_xattn_seq_d1_seqx_r2_3eac05'

def setup_inputs(seed: int=0):
    np.random.seed(seed)
    _w = jnp.asarray

    def _rec_inputs():
        import jax
        import jax.numpy as jnp
        _rk = jax.random.key(seed)
        x = 7.22e-05 + 1 * jax.random.normal(jax.random.fold_in(_rk, 1), (4, 1024, 1024), jnp.float32)
        _lenS = 1024 - jax.random.randint(jax.random.fold_in(_rk, 7), (4,), 0, max(1, 1024 // 4) + 1, jnp.int32)
        _lenS2 = 1024 - jax.random.randint(jax.random.fold_in(_rk, 8), (4,), 0, max(1, 1024 // 4) + 1, jnp.int32)
        _ctx_2048P = jax.random.normal(jax.random.fold_in(_rk, 11), (4, 16, 1024), jnp.float32)
        _ctx_2048c = jax.random.dirichlet(jax.random.fold_in(_rk, 511), 0.3 * jnp.ones((16,), jnp.float32), (4, 1024))
        _ctx_2048t = jnp.einsum('bsk,bkd->bsd', _ctx_2048c, _ctx_2048P)
        _ctx_2048t = _ctx_2048t * jax.lax.rsqrt(jnp.mean(jnp.square(_ctx_2048t)) + 1e-12) * 0.953939
        ctx_2048 = 4.13588e-05 + 0.999923 * (_ctx_2048t + 0.3 * jax.random.normal(jax.random.fold_in(_rk, 611), (4, 1024, 1024), jnp.float32))
        _validS = jnp.arange(1024)[None, :] < _lenS[:, None]
        _validS2 = jnp.arange(1024)[None, :] < _lenS2[:, None]
        _causal = jnp.tril(jnp.ones((1024, 1024), dtype=bool))
        mask_Bx1xSxS2_ff0 = jnp.where(jnp.ones((4, 1, 1024, 1024), dtype=bool), 0.0, -1000000000.0).astype(jnp.float32)
        return (x, ctx_2048, mask_Bx1xSxS2_ff0)
    x, ctx_2048, mask_Bx1xSxS2_ff0 = _rec_inputs()

    def _L0_xattn_setup():
        import jax, jax.numpy as jnp
        import numpy as np
        H = 1024
        NH = 32
        KVH = 8
        HD = H // NH
        GROUPS = NH // KVH
        EPS = 1e-06
        B, L, S = (4, 512, 512)

        def _gqa_forward(hidden_state, encoder_hidden_state, encoder_attention_mask, Wq, bq, Wk, bk, Wv, bv, Wo, bo, gamma, beta):
            b, l, _ = hidden_state.shape
            s = encoder_hidden_state.shape[1]
            q = hidden_state @ Wq + bq
            k = encoder_hidden_state @ Wk + bk
            v = encoder_hidden_state @ Wv + bv
            q = q.reshape(b, l, KVH, GROUPS, HD).transpose(0, 2, 3, 1, 4)
            k = k.reshape(b, s, KVH, HD).transpose(0, 2, 1, 3)
            v = v.reshape(b, s, KVH, HD).transpose(0, 2, 1, 3)
            scale = 1.0 / jnp.sqrt(jnp.asarray(HD, q.dtype))
            scores = jnp.einsum('bkgld,bksd->bkgls', q, k) * scale
            scores = scores + encoder_attention_mask[:, :, None, :, :]
            attn = jax.nn.softmax(scores, axis=-1)
            out = jnp.einsum('bkgls,bksd->bkgld', attn, v)
            out = out.transpose(0, 3, 1, 2, 4).reshape(b, l, H)
            out = out @ Wo + bo
            x = out + hidden_state
            mu = jnp.mean(x, axis=-1, keepdims=True)
            var = jnp.var(x, axis=-1, keepdims=True)
            return (x - mu) * jax.lax.rsqrt(var + EPS) * gamma + beta
        key = jax.random.key(seed)
        ks = jax.random.split(key, 12)
        sd = 0.02
        return {'hidden_state': jax.random.normal(ks[0], (B, L, H), jnp.float32), 'encoder_hidden_state': jax.random.normal(ks[1], (B, S, H), jnp.float32), 'encoder_attention_mask': jnp.zeros((B, 1, L, S), jnp.float32), 'Wq': jax.random.normal(ks[2], (H, H), jnp.float32) * sd, 'bq': jnp.zeros((H,), jnp.float32), 'Wk': jax.random.normal(ks[3], (H, KVH * HD), jnp.float32) * sd, 'bk': jnp.zeros((KVH * HD,), jnp.float32), 'Wv': jax.random.normal(ks[4], (H, KVH * HD), jnp.float32) * sd, 'bv': jnp.zeros((KVH * HD,), jnp.float32), 'Wo': jax.random.normal(ks[5], (H, H), jnp.float32) * sd, 'bo': jnp.zeros((H,), jnp.float32), 'gamma': jnp.ones((H,), jnp.float32), 'beta': jnp.zeros((H,), jnp.float32)}
    _L0_xattn_all = _L0_xattn_setup()
    _L0_xattn_in = {k: v for k, v in _L0_xattn_all.items() if k in ('Wq', 'bq', 'Wk', 'bk', 'Wv', 'bv', 'Wo', 'bo', 'gamma', 'beta')}
    del _L0_xattn_all
    return {'x': x, 'ctx_2048': ctx_2048, 'mask_Bx1xSxS2_ff0': mask_Bx1xSxS2_ff0, 'L0_xattn_Wq': _L0_xattn_in['Wq'], 'L0_xattn_bq': _L0_xattn_in['bq'], 'L0_xattn_Wk': _L0_xattn_in['Wk'], 'L0_xattn_bk': _L0_xattn_in['bk'], 'L0_xattn_Wv': _L0_xattn_in['Wv'], 'L0_xattn_bv': _L0_xattn_in['bv'], 'L0_xattn_Wo': _L0_xattn_in['Wo'], 'L0_xattn_bo': _L0_xattn_in['bo'], 'L0_xattn_gamma': _L0_xattn_in['gamma'], 'L0_xattn_beta': _L0_xattn_in['beta']}

def reference(x, ctx_2048, mask_Bx1xSxS2_ff0, L0_xattn_Wq, L0_xattn_bq, L0_xattn_Wk, L0_xattn_bk, L0_xattn_Wv, L0_xattn_bv, L0_xattn_Wo, L0_xattn_bo, L0_xattn_gamma, L0_xattn_beta):
    import jax
    import jax.numpy as jnp

    def _L0_xattn_ref(hidden_state, encoder_hidden_state, encoder_attention_mask, Wq, bq, Wk, bk, Wv, bv, Wo, bo, gamma, beta):
        import jax, jax.numpy as jnp
        import numpy as np
        H = 1024
        NH = 32
        KVH = 8
        HD = H // NH
        GROUPS = NH // KVH
        EPS = 1e-06
        B, L, S = (4, 512, 512)

        def _gqa_forward(hidden_state, encoder_hidden_state, encoder_attention_mask, Wq, bq, Wk, bk, Wv, bv, Wo, bo, gamma, beta):
            b, l, _ = hidden_state.shape
            s = encoder_hidden_state.shape[1]
            q = hidden_state @ Wq + bq
            k = encoder_hidden_state @ Wk + bk
            v = encoder_hidden_state @ Wv + bv
            q = q.reshape(b, l, KVH, GROUPS, HD).transpose(0, 2, 3, 1, 4)
            k = k.reshape(b, s, KVH, HD).transpose(0, 2, 1, 3)
            v = v.reshape(b, s, KVH, HD).transpose(0, 2, 1, 3)
            scale = 1.0 / jnp.sqrt(jnp.asarray(HD, q.dtype))
            scores = jnp.einsum('bkgld,bksd->bkgls', q, k) * scale
            scores = scores + encoder_attention_mask[:, :, None, :, :]
            attn = jax.nn.softmax(scores, axis=-1)
            out = jnp.einsum('bkgls,bksd->bkgld', attn, v)
            out = out.transpose(0, 3, 1, 2, 4).reshape(b, l, H)
            out = out @ Wo + bo
            x = out + hidden_state
            mu = jnp.mean(x, axis=-1, keepdims=True)
            var = jnp.var(x, axis=-1, keepdims=True)
            return (x - mu) * jax.lax.rsqrt(var + EPS) * gamma + beta
        return _gqa_forward(hidden_state, encoder_hidden_state, encoder_attention_mask, Wq, bq, Wk, bk, Wv, bv, Wo, bo, gamma, beta)
    x = _L0_xattn_ref(x, ctx_2048, mask_Bx1xSxS2_ff0, L0_xattn_Wq, L0_xattn_bq, L0_xattn_Wk, L0_xattn_bk, L0_xattn_Wv, L0_xattn_bv, L0_xattn_Wo, L0_xattn_bo, L0_xattn_gamma, L0_xattn_beta)
    return x

_drawn_inputs = setup_inputs


def setup_inputs(seed=0):
    import zlib

    import numpy as np

    out = dict(_drawn_inputs(seed))
    spreads = {'L0_xattn_bq': (0.0, 0.8),
     'L0_xattn_bk': (0.0, 0.8),
     'L0_xattn_bv': (0.0, 0.1),
     'L0_xattn_bo': (0.0, 0.1),
     'L0_xattn_gamma': (1.0, 0.2),
     'L0_xattn_beta': (0.0, 0.1)}
    factors = {}
    for name, (base, spread) in spreads.items():
        noise = np.random.default_rng([zlib.crc32(name.encode()), seed]).standard_normal(out[name].shape)
        drawn = base * np.exp(spread * noise) if base else spread * noise
        out[name] = jnp.asarray(drawn.astype(out[name].dtype))
    for name, factor in factors.items():
        out[name] = (out[name] * factor).astype(out[name].dtype)
    return out
```

```python
from contextlib import ExitStack

import concourse.bass as bass
from concourse import mybir

F32 = mybir.dt.float32
F32R = mybir.dt.float32r
BF16 = mybir.dt.bfloat16
I32 = mybir.dt.int32
ALU = mybir.AluOpType
ACT = mybir.ActivationFunctionType
AX = mybir.AxisListType

P = 128
B, L, H = 4, 1024, 1024
KVH, HEADS = 8, 4
D = H // (KVH * HEADS)
E = KVH * D
SCALE = float(D) ** -0.5
EPS = 1e-6
CH = 512
NCH = B * L // CH
HALVES = L // CH
CT = H // P
TT = CH // P
NG = B * KVH
ST = L // P
PAIRS = NG // 2
LOWEST = -3.4028234663852886e38


def wait(engine, semaphore, value):
    if not isinstance(value, int) or value > 0:
        engine.wait_ge(semaphore, value)


def wait_before(engine, semaphore, value, counter):
    wait(engine, semaphore, value)
    engine.sem_inc(counter, 1)


def f32(ap):
    return ap.bitcast(F32)



def project_qkv(nc, x, ctx_in, mask, wq, bq, wk, bk, wv, bv, ident_dram, scratch, flags):
    x_v = x.rearrange("b (n t p) c -> (b n) p t c", t=TT, p=P)
    c_v = ctx_in.rearrange("b (n t p) c -> (b n) p t c", t=TT, p=P)
    m_v = mask.rearrange("b o (n t p) s -> (b o n) p t s", t=TT, p=P)
    wq_v = wq.rearrange("(k p) n -> p k n", p=P)
    wk_v = wk.rearrange("(k p) n -> p k n", p=P)
    wv_v = wv.rearrange("(k p) n -> p k n", p=P)
    v_v = scratch["v"].rearrange("(i t p) e -> i t p e", t=TT, p=P)
    q_hi_v, q_lo_v = scratch["q_hi"], scratch["q_lo"]
    k_hi_v, k_lo_v = scratch["k_hi"], scratch["k_lo"]

    with ExitStack() as st:
        sb = lambda name, shape, dt: st.enter_context(nc.sbuf_tensor(name, shape, dt))
        sem = lambda name: st.enter_context(nc.semaphore(name))
        x_tok = sb("x_tok", [P, TT, H], F32)
        c_tok = sb("c_tok", [P, TT, H], F32)
        m_tok = sb("m_tok", [P, TT, H], F32)
        xT_hi, xT_lo = sb("xT_hi", [P, CT, CH], F32R), sb("xT_lo", [P, CT, CH], F32R)
        cT_hi, cT_lo = sb("cT_hi", [P, CT, CH], F32R), sb("cT_lo", [P, CT, CH], F32R)
        wq_hi, wq_lo = sb("wq_hi", [P, CT, H], F32R), sb("wq_lo", [P, CT, H], F32R)
        wk_hi, wk_lo = sb("wk_hi", [P, CT, E], F32R), sb("wk_lo", [P, CT, E], F32R)
        wv_hi, wv_lo = sb("wv_hi", [P, CT, E], F32R), sb("wv_lo", [P, CT, E], F32R)
        out_hi, out_lo = sb("qk_out_hi", [P, 2, CH], F32R), sb("qk_out_lo", [P, 2, CH], F32R)
        v_out = sb("v_out", [P, 2, E], F32)
        ident = sb("ident1", [P, P], F32)
        ones = sb("ones1", [P, P], F32)
        bq_c = sb("bq_c", [P, CT], F32)
        bk_c = sb("bk_c", [P, 2], F32)
        bks_c = sb("bks_c", [P, 2], F32)
        bv_r = sb("bv_r", [P, E], F32)
        absum = sb("absum", [P, NCH], F32)
        bsum = sb("bsum", [P, B], F32)
        tr = [st.enter_context(nc.psum_tensor(f"tr{i}", [P, CH], F32)) for i in range(2)]
        pq = [st.enter_context(nc.psum_tensor(f"pq{i}", [P, CH], F32)) for i in range(4)]
        pkv = [st.enter_context(nc.psum_tensor(f"pkv{i}", [P, CH], F32)) for i in range(2)]

        x_loaded, c_loaded, m_loaded = sem("x_loaded"), sem("c_loaded"), sem("m_loaded")
        w_loaded = [sem(f"w_loaded{i}") for i in range(3)]
        consts_loaded = sem("consts_loaded")
        w_hi, w_lo = sem("w_hi"), sem("w_lo")
        tr_ready, tr_hi, tr_lo = sem("tr_ready"), sem("tr_hi"), sem("tr_lo")
        out_ready, hi_done, out_done = sem("out_ready"), sem("hi_done"), sem("out_done")
        qk_stored = [sem(f"qk_stored{i}") for i in range(2)]
        v_stored = [sem(f"v_stored{i}") for i in range(2)]
        mask_summed, small_done, flag_ready = sem("mask_summed"), sem("small_done"), sem("flag_ready")
        ones_set = sem("ones_set")

        T, OUT, QK, V = 2 * CT, 14, 10, 4
        tr_ctx = lambda i, k: CT + T * i + k
        tr_x = lambda i, k: T * i + k

        def steps(last):
            for m in range(CT):
                yield "tc", m
                yield "q", m
            x_at = [(0, 1), (2, 3), (4,), (5,), (6,), (7,)]
            for n in range(6):
                yield ("k", n) if n < 2 else ("v", n - 2)
                if not last:
                    for k in x_at[n]:
                        yield "tx", k

        def iterations(engine, body):
            body(0, False)
            with engine.Fori(1, NCH - 1) as i:
                body(i, False)
            body(NCH - 1, True)

        block = st.enter_context(nc.Block())

        @block.sync
        def _(sp):
            sp.dma_start(ident[:], ident_dram).then_inc(consts_loaded, 16)
            sp.dma_start(x_tok[:], x_v[0]).then_inc(x_loaded, 16)
            sp.dma_start(c_tok[:], wq_v[:, 0:4, :]).then_inc(w_loaded[0], 16)
            sp.dma_start(m_tok[:], wq_v[:, 4:8, :]).then_inc(w_loaded[1], 16)
            sp.dma_start(bq_c[:], bq.rearrange("(m p) -> p m", p=P), allow_slow_non_contiguous=True).then_inc(consts_loaded, 16)
            sp.dma_start(bk_c[:], bk.rearrange("(m p) -> p m", p=P), allow_slow_non_contiguous=True).then_inc(consts_loaded, 16)
            sp.dma_start(bv_r[:], bv.partition_broadcast(P)).then_inc(consts_loaded, 16)
            sp.wait_ge(tr_ready, CT)
            wkv = x_tok[:].rearrange("p t c -> p (t c)").rearrange("p (w k e) -> p w k e", w=2, e=E)
            sp.dma_start(wkv[:, 0], wk_v).then_inc(w_loaded[2], 16)
            sp.dma_start(wkv[:, 1], wv_v).then_inc(w_loaded[2], 16)
            sp.wait_ge(w_lo, 4)
            sp.dma_start(c_tok[:], c_v[0]).then_inc(c_loaded, 16)
            sp.wait_ge(w_lo, 8)
            sp.dma_start(m_tok[:], m_v[0]).then_inc(m_loaded, 16)
            sp.wait_ge(w_lo, 10)

            def body(i, last):
                if not last:
                    wait(sp, tr_ready, tr_x(i, CT))
                    sp.dma_start(x_tok[:], x_v[bass.ds(i + 1, 1)].rearrange("o p t c -> (o p) t c")).then_inc(x_loaded, 16)
                for what, n in steps(last):
                    if what in "qk":
                        j = n if what == "q" else CT + n
                        wait(sp, out_done, OUT * i + j + 1)
                        hi, lo = (q_hi_v, q_lo_v) if what == "q" else (k_hi_v, k_lo_v)
                        for part, dram in ((out_hi, hi), (out_lo, lo)):
                            to = dram[bass.ds(i, 1), n] if what == "q" else dram[bass.ds(i, 1), n * P:(n + 1) * P]
                            sp.dma_start(to.rearrange("o p l -> (o p) l"), f32(part[:, j % 2])).then_inc(qk_stored[j % 2], 16)
                    if what == "v":
                        wait(sp, out_done, OUT * i + QK + n + 1)
                        sp.dma_start(v_v[bass.ds(i, 1), n].rearrange("o p e -> (o p) e"), v_out[:, n % 2]).then_inc(v_stored[n % 2], 16)
                    if what == "q" and n == CT - 1 and not last:
                        wait(sp, tr_ready, tr_ctx(i, CT))
                        sp.dma_start(c_tok[:], c_v[bass.ds(i + 1, 1)].rearrange("o p t c -> (o p) t c")).then_inc(c_loaded, 16)
                    if what == "k" and n == 0 and not last:
                        wait(sp, mask_summed, i + 1)
                        sp.dma_start(m_tok[:], m_v[bass.ds(i + 1, 1)].rearrange("o p t c -> (o p) t c")).then_inc(m_loaded, 16)
            iterations(sp, body)
            for r in range(2):
                sp.wait_ge(qk_stored[r], NCH * QK // 2 * 32)
                sp.wait_ge(v_stored[r], NCH * V // 2 * 16)

        @block.tensor
        def _(pe):
            def transpose_tile(tok, at, k):
                wait(pe, tr_lo, at - 1)
                for t in range(TT):
                    last = nc.tensor.transpose(tr[k % 2][:, t * P:(t + 1) * P], tok[:, t, k * P:(k + 1) * P], ident[:])
                last.then_inc(tr_ready, 1)

            def product(bank, terms):
                for n, (a, b) in enumerate(terms):
                    last = nc.tensor.matmul(bank, a, b, start=n == 0, stop=n == len(terms) - 1)
                last.then_inc(out_ready, 1)

            pe.wait_ge(consts_loaded, 64)
            pe.wait_ge(x_loaded, 16)
            for k in range(CT):
                transpose_tile(x_tok, k, k)

            def body(i, last):
                for what, n in steps(last):
                    if what == "tc":
                        if n == 0:
                            wait(pe, c_loaded, 16 * (i + 1))
                        transpose_tile(c_tok, tr_ctx(i, n), n)
                    if what == "tx":
                        if n == 0:
                            wait(pe, x_loaded, 16 * (i + 2))
                        transpose_tile(x_tok, tr_x(i + 1, n), n)
                    if what == "q":
                        if n == 0:
                            wait(pe, tr_lo, tr_x(i, CT))
                            if isinstance(i, int):
                                wait(pe, w_lo, 8)
                        wait(pe, out_done, OUT * i + n - 3 if n >= 4 else OUT * (i - 1) + n + 5)
                        cols = slice(n * P, (n + 1) * P)
                        product(pq[n % 4][:], [(w[:, k, cols], t[:, k]) for k in range(CT)
                                               for w, t in ((wq_hi, xT_hi), (wq_lo, xT_hi), (wq_hi, xT_lo))])
                    if what == "k":
                        if n == 0:
                            wait(pe, tr_lo, tr_ctx(i, CT))
                            if isinstance(i, int):
                                wait(pe, w_lo, 10)
                        wait(pe, out_done, OUT * i + n - 1)
                        cols = slice(n * P, (n + 1) * P)
                        product(pkv[n % 2][:], [(w[:, k, cols], t[:, k]) for k in range(CT)
                                                for w, t in ((wk_hi, cT_hi), (wk_lo, cT_hi), (wk_hi, cT_lo))])
                    if what == "v":
                        wait(pe, out_done, OUT * i + CT + n + 1)
                        cols = slice(n * P, (n + 1) * P)
                        product(pkv[n % 2][:, 0:E], [(t[:, k, cols], w[:, k]) for k in range(CT)
                                                     for w, t in ((wv_hi, cT_hi), (wv_lo, cT_hi), (wv_hi, cT_lo))])
            iterations(pe, body)
            pe.wait_ge(ones_set, 1)
            pe.wait_ge(mask_summed, NCH)
            nc.tensor.matmul(tr[0][:, 0:NCH], ones[:], absum[:], start=True, stop=True).then_inc(flag_ready, 1)

        @block.scalar
        def _(act):
            def transposed(at, k, hi):
                wait(act, tr_ready, at + 1)
                nc.scalar.activation(hi[:, k], tr[k % 2][:], ACT.Copy).then_inc(tr_hi, 1)

            act.wait_ge(x_loaded, 16)
            for k in range(CT):
                transposed(k, k, xT_hi)
            for k in range(CT):
                src = (c_tok, m_tok)[k // 4]
                act.wait_ge(w_loaded[k // 4], 16)
                nc.scalar.activation(wq_hi[:, k], src[:, k % 4], ACT.Copy).then_inc(w_hi, 1)
            wkv = x_tok[:].rearrange("p t c -> p (t c)").rearrange("p (w k e) -> p w k e", w=2, e=E)
            act.wait_ge(w_loaded[2], 32)
            nc.scalar.activation(wk_hi[:], wkv[:, 0], ACT.Copy, scale=SCALE).then_inc(w_hi, 1)
            nc.scalar.activation(wv_hi[:], wkv[:, 1], ACT.Copy).then_inc(w_hi, 1)
            act.wait_ge(small_done, 1)

            def body(i, last):
                for what, n in steps(last):
                    if what == "tc":
                        if n == 0:
                            wait(act, out_ready, OUT * i)
                        transposed(tr_ctx(i, n), n, cT_hi)
                    if what == "tx":
                        if n == 0:
                            wait(act, out_ready, OUT * i + CT)
                        transposed(tr_x(i + 1, n), n, xT_hi)
                    if what in "qk":
                        j = n if what == "q" else CT + n
                        bank, bias = (pq[n % 4], bq_c) if what == "q" else (pkv[n % 2], bks_c)
                        wait(act, out_ready, OUT * i + j + 1)
                        wait(act, qk_stored[j % 2], 32 * (QK // 2 * i + j // 2))
                        nc.scalar.activation(out_hi[:, j % 2], bank[:], ACT.Identity, bias=bias[:, n:n + 1]).then_inc(hi_done, 1)
            iterations(act, body)

        @block.vector
        def _(dve):
            def transposed(at, k, hi, lo):
                wait(dve, tr_hi, at + 1)
                nc.vector.tensor_tensor(lo[:, k], tr[k % 2][:], f32(hi[:, k]), ALU.subtract).then_inc(tr_lo, 1)

            nc.vector.memset(ones[:], 1.0).then_inc(ones_set, 1)
            for k in range(CT):
                transposed(k, k, xT_hi, xT_lo)
            for k in range(CT):
                src = (c_tok, m_tok)[k // 4]
                dve.wait_ge(w_hi, k + 1)
                nc.vector.tensor_tensor(wq_lo[:, k], src[:, k % 4], f32(wq_hi[:, k]), ALU.subtract).then_inc(w_lo, 1)
            wkv = x_tok[:].rearrange("p t c -> p (t c)").rearrange("p (w k e) -> p w (k e)", w=2, e=E)
            flat = lambda t: f32(t[:]).rearrange("p k e -> p (k e)")
            dve.wait_ge(w_hi, CT + 1)
            nc.vector.scalar_tensor_tensor(wk_lo[:].rearrange("p k e -> p (k e)"), wkv[:, 0], SCALE, flat(wk_hi),
                                           ALU.mult, ALU.subtract).then_inc(w_lo, 1)
            dve.wait_ge(w_hi, CT + 2)
            nc.vector.tensor_tensor(wv_lo[:].rearrange("p k e -> p (k e)"), wkv[:, 1], flat(wv_hi), ALU.subtract).then_inc(w_lo, 1)
            dve.wait_ge(consts_loaded, 64)
            nc.vector.tensor_scalar(bks_c[:], bk_c[:], SCALE, None, ALU.mult).then_inc(small_done, 1)
            dve.wait_ge(small_done, 1)

            def body(i, last):
                for what, n in steps(last):
                    if what == "tc":
                        transposed(tr_ctx(i, n), n, cT_hi, cT_lo)
                    if what == "tx":
                        transposed(tr_x(i + 1, n), n, xT_hi, xT_lo)
                    if what in "qk":
                        j = n if what == "q" else CT + n
                        bank, bias = (pq[n % 4], bq_c) if what == "q" else (pkv[n % 2], bks_c)
                        wait(dve, hi_done, QK * i + j + 1)
                        nc.vector.scalar_tensor_tensor(out_lo[:, j % 2], bank[:], bias[:, n:n + 1], f32(out_hi[:, j % 2]),
                                                       ALU.add, ALU.subtract).then_inc(out_done, 1)
                    if what == "v":
                        wait(dve, out_ready, OUT * i + QK + n + 1)
                        wait(dve, v_stored[n % 2], 16 * (V // 2 * i + n // 2))
                        nc.vector.tensor_tensor(v_out[:, n % 2], pkv[n % 2][:, 0:E], bv_r[:], ALU.add).then_inc(out_done, 1)
                    if what == "q" and n == CT - 1:
                        wait(dve, m_loaded, 16 * (i + 1))
                        nc.vector.tensor_reduce(absum[:, bass.ds(i, 1)], m_tok[:].rearrange("p t s -> p (t s)"), AX.X, ALU.add,
                                                apply_absolute_value=True).then_inc(mask_summed, 1)
            iterations(dve, body)
            dve.wait_ge(flag_ready, 1)
            halves = tr[0][:, 0:NCH].rearrange("p (b h) -> p b h", h=HALVES)
            nc.vector.tensor_reduce(bsum[:], halves, AX.X, ALU.add).then_inc(small_done, 1)
            dve.wait_ge(small_done, 2)
            per_batch = PAIRS // B
            nc.vector.tensor_scalar(flags[:].rearrange("p (b r) -> p b r", r=per_batch),
                                    bsum[:].unsqueeze(2).to_broadcast([P, B, per_batch]),
                                    0.0, None, ALU.not_equal).then_inc(small_done, 1)
            dve.wait_ge(small_done, 3)



def attend(nc, mask, ident_dram, scratch, flags):
    q_hi_v = scratch["q_hi"].rearrange("i g (h d) l -> i g d h l", d=D)
    q_lo_v = scratch["q_lo"].rearrange("i g (h d) l -> i g d h l", d=D)
    k_v = {part: scratch[part].rearrange("(b f) e s -> b e f s", f=HALVES) for part in ("k_hi", "k_lo")}
    v_v = scratch["v"].rearrange("(b t p) e -> b p t e", t=ST, p=P)
    o_v = scratch["o"]
    mask_v = mask.rearrange("b o (t p) s -> t (b o) p s", p=P)
    R3 = 3 * D
    R = R3 + 2
    STEPS = HALVES * ST
    SLOTS = ST
    HT = 2 * ST * HEADS
    ADDS = 5

    with ExitStack() as st:
        sb = lambda name, shape, dt: st.enter_context(nc.sbuf_tensor(name, shape, dt))
        ps = lambda name, shape: st.enter_context(nc.psum_tensor(name, shape, F32))
        sem = lambda name: st.enter_context(nc.semaphore(name))
        q_st = [[sb(f"q_st{u}{f}", [P, HEADS, CH], F32R) for f in range(HALVES)] for u in range(2)]
        k_max = [sb(f"k_max{u}", [P, L], F32R) for u in range(2)]
        k_exp = [sb(f"k_exp{u}", [P, L], F32R) for u in range(2)]
        v_sb = [sb(f"v_sb{u}", [P, ST, D], F32) for u in range(2)]
        mask_q = sb("mask_q", [P, ST, L], F32)
        mask_k = sb("mask_k", [P, ST, L], F32)
        probs = sb("probs", [P, SLOTS, HEADS, CH], F32)
        key_sum = [sb(f"key_sum{f}", [P, HEADS * CH], F32) for f in range(2)]
        sums_t, recip_row = sb("sums_t", [P, CH], F32), sb("recip_row", [P, CH // D], F32)
        recip, o_raw, o_n = sb("recip", [P, CH], F32), sb("o_raw", [P, CH], F32), sb("o_n", [P, CH], F32)
        junk = sb("junk", [P, 2, CH], BF16)
        half_max = sb("half_max", [P, 2, HEADS * ST], F32)
        row_max = sb("row_max", [P, HEADS * ST], F32)
        neg_max = sb("neg_max", [P, 4, HEADS * ST], F32R)
        neg_max_t = sb("neg_max_t", [2 * HEADS * ST, P], F32)
        ones = sb("ones2", [P, D], F32)
        ident = sb("ident2", [P, P], F32)
        sc_q = [ps(f"sc_q{i}", [P, CH]) for i in range(2)]
        sc_k = [ps(f"sc_k{i}", [P, 2 * CH]) for i in range(2)]
        out_ps = ps("out_ps", [P, CH])
        misc = ps("misc", [P, CH])

        consts_loaded, consts_set = sem("consts2_loaded"), sem("consts2_set")
        mask_loaded = [sem(f"mask_loaded{t}") for t in range(ST)]
        q_loaded = [[sem(f"q_loaded{u}{f}") for f in range(HALVES)] for u in range(2)]
        km_loaded = [sem(f"km_loaded{u}") for u in range(2)]
        kv_loaded = [sem(f"kv_loaded{u}") for u in range(2)]
        nm_loaded = [sem(f"nm_loaded{u}") for u in range(2)]
        q_scored, q_maxed = sem("q_scored"), sem("q_maxed")
        k_scored, k_masked, exp_done = sem("k_scored"), sem("k_masked"), sem("exp_done")
        pv_done, sums_done, key_added = sem("pv_done"), sem("sums_done"), sem("key_added")
        raw_out, sums_read, out_ready, o_stored = sem("raw_out"), sem("sums_read"), sem("o_ready"), sem("o_stored")
        max_split, max_turned, max_ready = sem("max_split"), sem("max_turned"), sem("max_ready")
        mk_turned, mk_ready = sem("mk_turned"), sem("mk_ready")
        seen = sem("seen2")
        chain, norm = sem("max_chain"), sem("norm_chain")

        SPREAD = 5
        rows_at = lambda s: list(range(min(SPREAD * s, HT), min(SPREAD * (s + 1), HT)))
        SUMS_AT, NORM_AT, SPLIT_AT, TURN_AT = 2, 4, 13, 14
        half_row = lambda a: (a // (2 * HEADS), a // 2 % HEADS, a % 2)

        def pairs(engine, body, begin=None):
            body(0, True, False)
            with engine.Fori(1, PAIRS - 1) as it:
                body(it, False, False)
            body(PAIRS - 1, False, True)

        block = st.enter_context(nc.Block())

        @block.sync
        def _(sp):
            sp.dma_start(ident[:], ident_dram).then_inc(consts_loaded, 16)

            def load_mask(t, b):
                sp.dma_start(mask_q[:, t], mask_v[t, bass.ds(b, 1)].rearrange("o p s -> (o p) s")).then_inc(mask_loaded[t], 16)

            def load_q(n, u, f):
                b, g = n // KVH, n % KVH
                for row, part in ((0, q_hi_v), (1, q_hi_v), (2, q_lo_v)):
                    src = part[bass.ds(b * HALVES + f, 1), bass.ds(g, 1)].rearrange("o r d h l -> (o r d) h l")
                    sp.dma_start(f32(q_st[u][f][row * D:(row + 1) * D]), src).then_inc(q_loaded[u][f], 16)

            def load_k(n, dst, semaphore):
                b, g = n // KVH, n % KVH
                for row, part in ((0, "k_hi"), (1, "k_lo"), (2, "k_hi")):
                    src = k_v[part][bass.ds(b, 1), bass.ds(g * D, D)].rearrange("o d f s -> (o d) f s")
                    sp.dma_start(f32(dst[row * D:(row + 1) * D]).rearrange("d (f s) -> d f s", f=HALVES), src).then_inc(semaphore, 16)

            def load_v(n, u):
                b, g = n // KVH, n % KVH
                src = v_v[bass.ds(b, 1), :, :, bass.ds(g * D, D)].rearrange("o p t e -> (o p) t e")
                sp.dma_start(v_sb[u][:], src).then_inc(kv_loaded[u], 16)

            def store_o(at, f):
                wait(sp, out_ready, at * HALVES + f + 1)
                b, g = at // KVH, at % KVH
                dst = o_v[bass.ds(b * HALVES + f, 1), bass.ds(g, 1)].rearrange("o r p l -> (o r p) l")
                sp.dma_start(dst, o_n[:]).then_inc(o_stored, 16)

            def store_max(n, u):
                wait(sp, max_ready, n + 1)
                for part in range(2):
                    for f in range(HALVES):
                        row, at = R3 + part, (part * HALVES + f) * 16
                        sp.dma_start(f32(q_st[u][f][row:row + 1]).rearrange("o h (t l) -> o (h t) l", l=P),
                                     neg_max_t[at:at + 16]).then_inc(nm_loaded[u], 16)

            load_q(0, 0, 0)
            load_k(0, k_max[0], km_loaded[0])
            load_mask(0, 0)
            load_q(0, 0, 1)
            for t in range(1, ST):
                load_mask(t, 0)
            load_q(1, 1, 0)
            load_k(1, k_max[1], km_loaded[1])
            load_k(0, k_exp[0], kv_loaded[0])
            load_v(0, 0)
            store_max(0, 0)

            def body(it, first, last):
                for u in range(2):
                    n = 2 * it + u
                    no_next = last and u == 1
                    if not no_next:
                        wait(sp, k_scored, 32 * n)
                        load_q(n + 1, 1 - u, 1)
                        load_k(n + 1, k_exp[1 - u], kv_loaded[1 - u])
                        wait(sp, pv_done, STEPS * n)
                        load_v(n + 1, 1 - u)
                    if not (first and u == 0):
                        store_o(n - 1, 1)
                    if not last:
                        wait(sp, k_scored, 32 * n + 16)
                        load_q(n + 2, u, 0)
                        wait(sp, q_maxed, HT * (n + 1))
                        load_k(n + 2, k_max[u], km_loaded[u])
                    store_o(n, 0)
                    if not no_next:
                        store_max(n + 1, 1 - u)
                    if u == 0 and not first and not last:
                        with sp.If((it % (PAIRS // B)) == PAIRS // B - 1):
                            for t in range(ST):
                                wait(sp, q_maxed, HT * (n + 1) + 2 * HEADS * (t + 1))
                                load_mask(t, (it + 1) // (PAIRS // B))
            pairs(sp, body)
            store_o(NG - 1, 1)
            sp.wait_ge(o_stored, 16 * NG * HALVES)

        @block.gpsimd
        def _(pool):
            def body(it, first, last):
                for u in range(2):
                    n = 2 * it + u
                    for f in range(HALVES):
                        half = HALVES * n + f
                        for k in range(ADDS):
                            wait(pool, exp_done, 32 * n + 2 * (ST * f + k + 2))
                            if k == 0:
                                wait(pool, sums_done, half - 1)
                            if k > 0:
                                wait(pool, key_added, ADDS * half + k)
                            flat = lambda s: probs[:, s].rearrange("p h l -> p (h l)")
                            nc.gpsimd.tensor_tensor(key_sum[f][:], flat(0) if k == 0 else key_sum[f][:], flat(k + 1),
                                                    ALU.add).then_inc(key_added, 1)
            pairs(pool, body)

        @block.tensor
        def _(pe):
            def score_q(n, turn, u, a):
                t, h, f = half_row(a)
                if a == 0:
                    wait(pe, km_loaded[u], 48 * (turn + 1))
                if a % HT == 0 or a == HT // 2:
                    wait(pe, q_loaded[u][t // (ST // 2)], 48 * (turn + 1))
                wait(pe, q_maxed, HT * n + a - 1)
                tl = t % (ST // 2)
                nc.tensor.matmul(sc_q[a % 2][:], q_st[u][t // (ST // 2)][0:R3, h, tl * P:(tl + 1) * P],
                                 k_max[u][0:R3, f * CH:(f + 1) * CH], start=True, stop=True).then_inc(q_scored, 1)

            def turn_max(n):
                wait(pe, max_split, n + 1)
                wait(pe, sums_read, HALVES * (n - 1) + 1)
                nc.tensor.transpose(misc[:, 0:P], f32(neg_max[:]).rearrange("p a c -> p (a c)"), ident[:]).then_inc(max_turned, 1)

            def score_k(n, u, s, pair):
                f, t = divmod(s, ST)
                wait(pe, exp_done, 32 * n + 2 * s + pair - 1)
                for hh in range(2):
                    last = nc.tensor.matmul(sc_k[pair][:, hh * CH:(hh + 1) * CH], k_exp[u][0:R, t * P:(t + 1) * P],
                                            q_st[u][f][0:R, 2 * pair + hh], start=True, stop=True)
                last.then_inc(k_scored, 1)

            def times_v(n, u, s):
                t = s % ST
                wait(pe, exp_done, 32 * n + 2 * s + 2)
                if t == 0:
                    wait(pe, raw_out, HALVES * n + s // ST)
                for h in range(HEADS):
                    last = nc.tensor.matmul(out_ps[h * D:(h + 1) * D], v_sb[u][:, t], probs[:, t, h],
                                            start=t == 0, stop=t == ST - 1, tile_position=(0, h * D))
                last.then_inc(pv_done, 1)

            def sum_keys(half, f):
                wait(pe, key_added, ADDS * (half + 1))
                parts = [probs[:, ST - 2], probs[:, ST - 1], key_sum[f][:].rearrange("p (h l) -> p h l", h=HEADS)]
                for j, part in enumerate(parts):
                    for h in range(HEADS):
                        last = nc.tensor.matmul(misc[h * D:(h + 1) * D], ones[:], part[:, h], start=j == 0,
                                                stop=j == len(parts) - 1, tile_position=(0, h * D))
                last.then_inc(sums_done, 1)

            def turn_mask(it):
                for t in range(ST):
                    wait(pe, mask_loaded[t], 16 * (it // (PAIRS // B) + 1))
                for j in range(2 * ST):
                    t, f = divmod(j, 2)
                    wait(pe, mk_ready, 2 * ST * it + j)
                    for r in range(4):
                        last = nc.tensor.transpose(misc[:, r * P:(r + 1) * P], mask_q[:, 4 * f + r, t * P:(t + 1) * P], ident[:])
                    last.then_inc(mk_turned, 1)

            pe.wait_ge(consts_loaded, 16)
            pe.wait_ge(consts_set, 4)
            for a in range(HT):
                if a % (2 * HEADS) == 0:
                    pe.wait_ge(mask_loaded[a // (2 * HEADS)], 16)
                score_q(0, 0, 0, a)
            turn_max(0)

            def body(it, first, last):
                has_mask = pe.value_load(flags[0:1, bass.ds(it, 1)], min_val=0, max_val=1)
                with pe.If(has_mask != 0):
                    wait(pe, sums_read, 2 * HALVES * it - 1)
                    wait(pe, max_ready, 2 * it + 1)
                    turn_mask(it)
                with pe.Else():
                    wait(pe, mk_turned, 2 * ST * it)
                    pe.sem_inc(mk_turned, 2 * ST)
                for u in range(2):
                    n = 2 * it + u
                    no_next = last and u == 1
                    for s in range(STEPS):
                        if s == 0:
                            wait(pe, kv_loaded[u], 64 * (it + 1))
                            wait(pe, nm_loaded[u], 64 * (it + 1))
                        score_k(n, u, s, 0)
                        rows = [] if no_next else rows_at(s)
                        for a in rows[:2]:
                            score_q(n + 1, it + u, 1 - u, a)
                        score_k(n, u, s, 1)
                        if s > 0:
                            times_v(n, u, s - 1)
                        elif not (first and u == 0):
                            times_v(n - 1, 1 - u, STEPS - 1)
                        for a in rows[2:]:
                            score_q(n + 1, it + u, 1 - u, a)
                        if s % ST == SUMS_AT and not (first and u == 0 and s < ST):
                            if s < ST:
                                wait(pe, max_ready, n + 1)
                            else:
                                wait(pe, sums_read, HALVES * n)
                            sum_keys(HALVES * n + s // ST - 1, (s // ST + 1) % 2)
                        if s == TURN_AT and not no_next:
                            turn_max(n + 1)
            pairs(pe, body)
            times_v(NG - 1, 1, STEPS - 1)
            wait(pe, sums_read, NG * HALVES - 1)
            sum_keys(NG * HALVES - 1, 1)

        @block.scalar
        def _(act):
            def exponentials(n, s, pair, masked):
                t = s % ST
                half = HALVES * n + s // ST
                c = 32 * n + 2 * s + pair + 1
                wait(act, k_masked if masked else k_scored, c)
                if not (isinstance(n, int) and n == 0 and s < ST):
                    wait(act, pv_done, STEPS * n + s - SLOTS + 1)
                    if t < ST - 2:
                        wait(act, key_added, ADDS * (half - 1) + max(t, 1))
                    else:
                        wait(act, sums_done, half)
                nc.scalar.activation(probs[:, t, 2 * pair:2 * pair + 2].rearrange("p h l -> p (h l)"), sc_k[pair][:],
                                     ACT.Exp).then_inc(exp_done, 1)

            def read_out(half):
                wait(act, pv_done, ST * (half + 1))
                wait(act, out_ready, half)
                nc.scalar.activation(o_raw[:], out_ps[:], ACT.Copy).then_inc(raw_out, 1)

            def read_max(n):
                wait(act, max_turned, n + 1)
                nc.scalar.activation(neg_max_t[:], misc[0:2 * HEADS * ST, 0:P], ACT.Copy).then_inc(max_ready, 1)

            read_max(0)

            def groups(it, first, last, masked):
                for u in range(2):
                    n = 2 * it + u
                    no_next = last and u == 1
                    for s in range(STEPS):
                        exponentials(n, s, 0, masked)
                        exponentials(n, s, 1, masked)
                        if s % ST == 0 and not (first and u == 0 and s == 0):
                            read_out(HALVES * n + s // ST - 1)
                        if s == TURN_AT and not no_next:
                            wait(act, nm_loaded[u], 64 * (it + 1))
                            read_max(n + 1)

            def body(it, first, last):
                has_mask = act.value_load(flags[0:1, bass.ds(it, 1)], min_val=0, max_val=1)
                with act.If(has_mask != 0):
                    for j in range(2 * ST):
                        t, f = divmod(j, 2)
                        wait(act, mk_turned, 2 * ST * it + j + 1)
                        if j == 0:
                            wait(act, k_masked, 64 * it)
                        nc.scalar.activation(mask_k[:, t, f * CH:(f + 1) * CH], misc[:], ACT.Copy).then_inc(mk_ready, 1)
                    groups(it, first, last, True)
                with act.Else():
                    wait(act, mk_ready, 2 * ST * it)
                    act.sem_inc(mk_ready, 2 * ST)
                    groups(it, first, last, False)
            pairs(act, body)
            read_out(NG * HALVES - 1)

        @block.vector
        def _(dve):
            nc.vector.memset(ones[:], 1.0).then_inc(consts_set, 1)
            nc.vector.memset(f32(neg_max[:, 2:4]), 0.0).then_inc(consts_set, 1)
            for u in range(2):
                nc.vector.memset(f32(k_exp[u][R3:R]), 1.0).then_inc(consts_set, 1)

            def maximum(n, batch, a):
                t, h, f = half_row(a)
                if a % (2 * HEADS) == 0:
                    wait(dve, mask_loaded[t], 16 * (batch + 1))
                wait_before(dve, q_scored, HT * n + a + 1, seen)
                c = (t // (ST // 2) * HEADS + h) * (ST // 2) + t % (ST // 2)
                nc.vector.tensor_tensor_reduce(out=junk[:, a % 2], in0=sc_q[a % 2][:], in1=mask_q[:, t, f * CH:(f + 1) * CH],
                                               scale=1.0, scalar=LOWEST, op0=ALU.add, op1=ALU.max,
                                               accum_out=half_max[:, f, c:c + 1]).then_inc(q_maxed, 1)

            def split_max(n):
                wait(dve, q_maxed, HT * (n + 1))
                nc.vector.tensor_tensor(row_max[:], half_max[:, 0], half_max[:, 1], ALU.max).then_inc(chain, 1)
                wait(dve, chain, 2 * n + 1)
                wait(dve, max_turned, n)
                nc.vector.tensor_scalar(neg_max[:, 0], row_max[:], -1.0, None, ALU.mult).then_inc(chain, 1)
                wait(dve, chain, 2 * n + 2)
                nc.vector.scalar_tensor_tensor(neg_max[:, 1], row_max[:], -1.0, f32(neg_max[:, 0]), ALU.mult,
                                               ALU.subtract).then_inc(max_split, 1)

            def normalize(half):
                wait(dve, sums_done, half + 1)
                nc.vector.transpose(sums_t[:], misc[:]).then_inc(sums_read, 1)
                wait(dve, sums_read, half + 1)
                nc.vector.reciprocal(recip_row[:], sums_t[:].rearrange("p (j c) -> p j c", c=D)[:, :, 0]).then_inc(norm, 1)
                wait(dve, norm, 2 * half + 1)
                nc.vector.transpose(recip[:], recip_row[:].unsqueeze(2).to_broadcast([P, CH // D, D])).then_inc(norm, 1)
                wait(dve, norm, 2 * half + 2)
                wait(dve, raw_out, half + 1)
                wait(dve, o_stored, 16 * half)
                nc.vector.tensor_tensor(o_n[:], o_raw[:], recip[:], ALU.mult).then_inc(out_ready, 1)

            def add_mask(n, s, pair):
                f, t = divmod(s, ST)
                wait(dve, k_scored, 32 * n + 2 * s + pair + 1)
                sc = sc_k[pair][:].rearrange("p (h l) -> p h l", h=2)
                m = mask_k[:, t, f * CH:(f + 1) * CH].unsqueeze(1).to_broadcast([P, 2, CH])
                nc.vector.tensor_tensor(sc, sc, m, ALU.add).then_inc(k_masked, 1)

            for a in range(HT):
                maximum(0, 0, a)
            split_max(0)

            def groups(it, first, last, masked):
                for u in range(2):
                    n = 2 * it + u
                    no_next = last and u == 1
                    batch_next = (it + u) // (PAIRS // B)
                    for s in range(STEPS):
                        rows = [] if no_next else rows_at(s)
                        if masked:
                            add_mask(n, s, 0)
                        for a in rows[:2]:
                            maximum(n + 1, batch_next, a)
                        if masked:
                            add_mask(n, s, 1)
                        for a in rows[2:]:
                            maximum(n + 1, batch_next, a)
                        if s % ST == NORM_AT and not (first and u == 0 and s < ST):
                            normalize(HALVES * n + s // ST - 1)
                        if s == SPLIT_AT and not no_next:
                            split_max(n + 1)

            def body(it, first, last):
                has_mask = dve.value_load(flags[0:1, bass.ds(it, 1)], min_val=0, max_val=1)
                with dve.If(has_mask != 0):
                    wait(dve, mk_ready, 2 * ST * (it + 1))
                    groups(it, first, last, True)
                with dve.Else():
                    wait(dve, k_masked, 64 * it)
                    dve.sem_inc(k_masked, 64)
                    groups(it, first, last, False)
            pairs(dve, body)
            normalize(NG * HALVES - 1)



def project_out(nc, x, wo, bo, gamma, beta, scratch, out):
    o_v = scratch["o"].rearrange("i g p l -> i p g l")
    x_v = x.rearrange("b (n t p) c -> (b n) p t c", t=TT, p=P)
    out_v = out.rearrange("b (n t p) c -> (b n) t p c", t=TT, p=P)
    wo_v = wo.rearrange("(k p) n -> p k n", p=P)
    STATS = nc.vector.BN_STATS_DIM
    NC = H // CH

    with ExitStack() as st:
        sb = lambda name, shape, dt: st.enter_context(nc.sbuf_tensor(name, shape, dt))
        sem = lambda name: st.enter_context(nc.semaphore(name))
        o_in = sb("o_in", [P, CT, CH], F32)
        oT_hi = [sb(f"oT_hi{i}", [P, CT, CH], F32R) for i in range(2)]
        oT_lo = [sb(f"oT_lo{i}", [P, CT, CH], F32R) for i in range(2)]
        x_res = [sb(f"x_res{i}", [P, TT, H], F32) for i in range(2)]
        wo_hi, wo_lo = sb("wo_hi", [P, CT, H], F32R), sb("wo_lo", [P, CT, H], F32R)
        bo_row, bo_hi, bo_lo = sb("bo_row", [1, H], F32), sb("bo_hi", [1, H], F32R), sb("bo_lo", [1, H], F32R)
        bo_two = sb("bo_two", [2, H], F32R)
        ones_f = sb("ones3f", [2, P], F32)
        ones = sb("ones3", [2, P], F32R)
        gamma_r, beta_r = sb("gamma_r", [P, H], F32), sb("beta_r", [P, H], F32)
        y, z = sb("y", [P, 2, H], F32), sb("z", [P, 2, H], F32)
        stats, mv = sb("stats", [P, NC, STATS], F32), sb("mv", [P, 2, 2], F32)
        std, rstd, shift = sb("std", [P, 2], F32), sb("rstd", [P, 2], F32), sb("shift", [P, 2], F32)
        eps = sb("eps", [P, 1], F32)
        acc = [st.enter_context(nc.psum_tensor(f"acc{i}", [P, H], F32)) for i in range(2)]

        w_loaded = [sem(f"wo_loaded{i}") for i in range(2)]
        o_loaded, bo_loaded, affine_loaded = sem("o_loaded"), sem("bo_loaded"), sem("affine_loaded")
        x_loaded = [sem(f"xr_loaded{i}") for i in range(2)]
        w_hi, w_lo, bo_split, bo_ready = sem("wo_hi_done"), sem("wo_lo_done"), sem("bo_split"), sem("bo_ready")
        ones_set, consts_set = sem("ones3_set"), sem("consts3_set")
        o_hi, o_lo = sem("o_hi"), sem("o_lo")
        projected, summed, measured, rooted = sem("projected"), sem("summed"), sem("measured"), sem("rooted")
        inverted, centred, scaled, done = sem("inverted"), sem("centred"), sem("scaled"), sem("done")
        statted, weighed, seen = sem("statted"), sem("weighed"), sem("seen3")
        stored = [sem(f"stored{i}") for i in range(2)]
        Q, QK = 4, CT // 4

        block = st.enter_context(nc.Block())

        @block.sync
        def _(sp):
            def load_o(c):
                sp.dma_start(o_in[:], o_v[bass.ds(c, 1)].rearrange("o p g l -> (o p) g l")).then_inc(o_loaded, 16)

            def load_x(c, r):
                sp.dma_start(x_res[r][:], x_v[bass.ds(c, 1)].rearrange("o p t c -> (o p) t c")).then_inc(x_loaded[r], 16)

            sp.dma_start(bo_row[:], bo.rearrange("(o n) -> o n", o=1)).then_inc(bo_loaded, 16)
            for i in range(2):
                sp.dma_start(x_res[i][:], wo_v[:, 4 * i:4 * i + 4, :]).then_inc(w_loaded[i], 16)
            load_o(0)
            sp.dma_start(gamma_r[:], gamma.partition_broadcast(P)).then_inc(affine_loaded, 16)
            sp.dma_start(beta_r[:], beta.partition_broadcast(P)).then_inc(affine_loaded, 16)
            sp.wait_ge(bo_split, 2)
            sp.dma_start(f32(bo_two[0:1]), f32(bo_hi[:])).then_inc(bo_ready, 16)
            sp.dma_start(f32(bo_two[1:2]), f32(bo_lo[:])).then_inc(bo_ready, 16)
            for i in range(2):
                sp.wait_ge(w_lo, 4 * (i + 1))
                load_x(i, i)

            def body(it, last):
                for r in range(2):
                    c = 2 * it + r
                    if not (last and r == 1):
                        wait(sp, o_lo, Q * (c + 1))
                        load_o(c + 1)
                    for t in range(TT):
                        k = TT * c + t
                        wait(sp, done, k + 1)
                        sp.dma_start(out_v[bass.ds(c, 1), t].rearrange("o p c -> (o p) c"), z[:, t % 2]).then_inc(stored[t % 2], 16)
                    if not last:
                        wait(sp, summed, TT * (c + 1))
                        load_x(c + 2, r)
            with sp.Fori(0, NCH // 2 - 1) as it:
                body(it, False)
            body(NCH // 2 - 1, True)
            for r in range(2):
                sp.wait_ge(stored[r], 16 * NCH * TT // 2)

        @block.tensor
        def _(pe):
            pe.wait_ge(bo_ready, 32)
            pe.wait_ge(ones_set, 2)
            pe.wait_ge(w_lo, CT)

            def body(it):
                for r in range(2):
                    c = 2 * it + r
                    for t in range(TT):
                        k = TT * c + t
                        if t == 0:
                            wait(pe, o_lo, Q * (c + 1))
                        wait(pe, summed, k - 1)
                        tok = slice(t * P, (t + 1) * P)
                        for n in range(NC):
                            cols = slice(n * CH, (n + 1) * CH)
                            bank = acc[t % 2][:, cols]
                            for g in range(CT):
                                for a, w in ((oT_hi[r], wo_hi), (oT_hi[r], wo_lo), (oT_lo[r], wo_hi)):
                                    nc.tensor.matmul(bank, a[:, g, tok], w[:, g, cols],
                                                     start=g == 0 and a is oT_hi[r] and w is wo_hi, stop=False)
                            last = nc.tensor.matmul(bank, ones[:], bo_two[:, cols], start=False, stop=True)
                        last.then_inc(projected, 1)
            body(0)
            with pe.Fori(1, NCH // 2) as it:
                body(it)

        @block.scalar
        def _(act):
            for k in range(CT):
                act.wait_ge(w_loaded[k // 4], 16)
                nc.scalar.activation(wo_hi[:, k], x_res[k // 4][:, k % 4], ACT.Copy).then_inc(w_hi, 1)
            act.wait_ge(bo_loaded, 16)
            nc.scalar.activation(bo_hi[:], bo_row[:], ACT.Copy).then_inc(bo_split, 1)
            act.wait_ge(ones_set, 1)
            nc.scalar.activation(ones[:], ones_f[:], ACT.Copy).then_inc(ones_set, 1)
            act.wait_ge(consts_set, 1)

            def split_hi(c, r, j):
                nc.scalar.activation(oT_hi[r][:, QK * j:QK * (j + 1)].rearrange("p g l -> p (g l)"),
                                     o_in[:, QK * j:QK * (j + 1)].rearrange("p g l -> p (g l)"), ACT.Copy).then_inc(o_hi, 1)

            act.wait_ge(o_loaded, 16)
            for j in range(Q):
                split_hi(0, 0, j)

            def body(it, last):
                for r in range(2):
                    c = 2 * it + r
                    for t in range(TT):
                        k = TT * c + t
                        wait(act, measured, k + 1)
                        nc.scalar.activation(std[:, t % 2:t % 2 + 1], mv[:, t % 2, 1:2], ACT.Sqrt, bias=eps[:]).then_inc(rooted, 1)
                        wait(act, centred, k + 1)
                        wait(act, stored[t % 2], 16 * (TT // 2 * c + t // 2))
                        nc.scalar.activation(z[:, t % 2], y[:, t % 2], ACT.Identity, scale=rstd[:, t % 2:t % 2 + 1],
                                             bias=shift[:, t % 2:t % 2 + 1]).then_inc(scaled, 1)
                        if not (last and r == 1):
                            if t == 0:
                                wait(act, o_loaded, 16 * (c + 2))
                                wait(act, projected, TT * c)
                            split_hi(c + 1, 1 - r, t)
            body(0, False)
            with act.Fori(1, NCH // 2 - 1) as it:
                body(it, False)
            body(NCH // 2 - 1, True)

        @block.vector
        def _(dve):
            nc.vector.memset(ones_f[:], 1.0).then_inc(ones_set, 1)
            nc.vector.memset(eps[:], EPS).then_inc(consts_set, 1)
            for k in range(CT):
                dve.wait_ge(w_hi, k + 1)
                nc.vector.tensor_tensor(wo_lo[:, k], x_res[k // 4][:, k % 4], f32(wo_hi[:, k]), ALU.subtract).then_inc(w_lo, 1)
            dve.wait_ge(bo_split, 1)
            nc.vector.tensor_tensor(bo_lo[:], bo_row[:], f32(bo_hi[:]), ALU.subtract).then_inc(bo_split, 1)

            def split_lo(c, r, j):
                flat = lambda a: a[:, QK * j:QK * (j + 1)].rearrange("p g l -> p (g l)")
                wait(dve, o_hi, Q * c + j + 1)
                nc.vector.tensor_tensor(flat(oT_lo[r]), flat(o_in), f32(flat(oT_hi[r])), ALU.subtract).then_inc(o_lo, 1)

            for j in range(Q):
                split_lo(0, 0, j)
            dve.wait_ge(affine_loaded, 32)

            def body(it, last):
                for r in range(2):
                    c = 2 * it + r
                    for t in range(TT):
                        k, s = TT * c + t, t % 2
                        if t == 0:
                            wait(dve, x_loaded[r], 16 * (it + 1))
                        wait(dve, projected, k + 1)
                        nc.vector.tensor_tensor(y[:, s], acc[s][:], x_res[r][:, t], ALU.add).then_inc(summed, 1)
                        wait(dve, summed, k + 1)
                        for n in range(NC):
                            nc.vector.bn_stats(stats[:, n], y[:, s, n * CH:(n + 1) * CH]).then_inc(statted, 1)
                        wait_before(dve, statted, NC * (k + 1), seen)
                        nc.vector.bn_aggr(mv[:, s], stats[:].rearrange("p n s -> p (n s)")).then_inc(measured, 1)
                        wait(dve, rooted, k + 1)
                        nc.vector.reciprocal(rstd[:, s:s + 1], std[:, s:s + 1]).then_inc(inverted, 1)
                        wait(dve, inverted, k + 1)
                        nc.vector.tensor_scalar(shift[:, s:s + 1], mv[:, s, 0:1], rstd[:, s:s + 1], -1.0, ALU.mult, ALU.mult).then_inc(centred, 1)
                        wait(dve, scaled, k + 1)
                        nc.vector.tensor_tensor(z[:, s], z[:, s], gamma_r[:], ALU.mult).then_inc(weighed, 1)
                        wait(dve, weighed, k + 1)
                        nc.vector.tensor_tensor(z[:, s], z[:, s], beta_r[:], ALU.add).then_inc(done, 1)
                        if not (last and r == 1):
                            split_lo(c + 1, 1 - r, t)
            with dve.Fori(0, NCH // 2 - 1) as it:
                body(it, False)
            body(NCH // 2 - 1, True)



_INS = ["x", "ctx_2048", "mask_Bx1xSxS2_ff0", "L0_xattn_Wq", "L0_xattn_bq", "L0_xattn_Wk", "L0_xattn_bk", "L0_xattn_Wv",
        "L0_xattn_bv", "L0_xattn_Wo", "L0_xattn_bo", "L0_xattn_gamma", "L0_xattn_beta"]


def cross_attention(nc, x, context, mask, wq, bq, wk, bk, wv, bv, wo, bo, gamma, beta, ident, out):
    dram = lambda name, shape: nc.dram_tensor(name, shape, F32, kind="Internal").ap()
    scratch = {"q_hi": dram("q_hi_s", [NCH, KVH, P, CH]), "q_lo": dram("q_lo_s", [NCH, KVH, P, CH]),
               "k_hi": dram("k_hi_s", [NCH, E, CH]), "k_lo": dram("k_lo_s", [NCH, E, CH]),
               "v": dram("v_s", [B * L, E]), "o": dram("o_s", [NCH, KVH, P, CH])}
    with nc.sbuf_tensor("flags", [P, PAIRS], I32) as flags:
        project_qkv(nc, x, context, mask, wq, bq, wk, bk, wv, bv, ident, scratch, flags)
        attend(nc, mask, ident, scratch, flags)
    project_out(nc, x, wo, bo, gamma, beta, scratch, out)


def kernel(**inputs):
    import numpy as _np
    import concourse.bacc as _bacc
    from concourse.bass_utils import run_bass_kernel_spmd as _run

    nc = _bacc.Bacc("TRN2", target_bir_lowering=False, num_devices=1, dynamic_dma_scratch_size=1024)
    arrays = {f"in_{name}": _np.ascontiguousarray(inputs[name]) for name in _INS}
    arrays["in_identity"] = _np.eye(P, dtype=_np.float32)
    args = [nc.dram_tensor(name, a.shape, mybir.dt.from_np(a.dtype), kind="ExternalInput").ap() for name, a in arrays.items()]
    out = nc.dram_tensor("out_0", (B, L, H), F32, kind="ExternalOutput").ap()
    cross_attention(nc, *args, out)
    result = _run(nc, [arrays], core_ids=[0])
    return result.results[0]["out_0"]
```

```python
from contextlib import ExitStack

import concourse.bass as bass
from concourse import mybir

F32 = mybir.dt.float32
F32R = mybir.dt.float32r
BF16 = mybir.dt.bfloat16
I32 = mybir.dt.int32
ALU = mybir.AluOpType
ACT = mybir.ActivationFunctionType
AX = mybir.AxisListType

P = 128
B, L, H = 4, 1024, 1024
KVH, HEADS = 8, 4
D = H // (KVH * HEADS)
E = KVH * D
SCALE = float(D) ** -0.5
EPS = 1e-6
CH = 512
NCH = B * L // CH
HALVES = L // CH
CT = H // P
TT = CH // P
NG = B * KVH
ST = L // P
PAIRS = NG // 2
LOWEST = -3.4028234663852886e38


def wait(engine, semaphore, value):
    if not isinstance(value, int) or value > 0:
        engine.wait_ge(semaphore, value)


def wait_before(engine, semaphore, value, counter):
    wait(engine, semaphore, value)
    engine.sem_inc(counter, 1)


def f32(ap):
    return ap.bitcast(F32)



def project_qkv(nc, x, ctx_in, mask, wq, bq, wk, bk, wv, bv, ident_dram, scratch, flags):
    x_v = x.rearrange("b (n t p) c -> (b n) p t c", t=TT, p=P)
    c_v = ctx_in.rearrange("b (n t p) c -> (b n) p t c", t=TT, p=P)
    m_v = mask.rearrange("b o (n t p) s -> (b o n) p t s", t=TT, p=P)
    wq_v = wq.rearrange("(k p) n -> p k n", p=P)
    wk_v = wk.rearrange("(k p) n -> p k n", p=P)
    wv_v = wv.rearrange("(k p) n -> p k n", p=P)
    v_v = scratch["v"].rearrange("(i t p) e -> i t p e", t=TT, p=P)
    q_hi_v, q_lo_v = scratch["q_hi"], scratch["q_lo"]
    k_hi_v, k_lo_v = scratch["k_hi"], scratch["k_lo"]

    with ExitStack() as st:
        sb = lambda name, shape, dt: st.enter_context(nc.sbuf_tensor(name, shape, dt))
        sem = lambda name: st.enter_context(nc.semaphore(name))
        x_tok = sb("x_tok", [P, TT, H], F32)
        c_tok = sb("c_tok", [P, TT, H], F32)
        m_tok = sb("m_tok", [P, TT, H], F32)
        xT_hi, xT_lo = sb("xT_hi", [P, CT, CH], F32R), sb("xT_lo", [P, CT, CH], F32R)
        cT_hi, cT_lo = sb("cT_hi", [P, CT, CH], F32R), sb("cT_lo", [P, CT, CH], F32R)
        wq_hi, wq_lo = sb("wq_hi", [P, CT, H], F32R), sb("wq_lo", [P, CT, H], F32R)
        wk_hi, wk_lo = sb("wk_hi", [P, CT, E], F32R), sb("wk_lo", [P, CT, E], F32R)
        wv_hi, wv_lo = sb("wv_hi", [P, CT, E], F32R), sb("wv_lo", [P, CT, E], F32R)
        out_hi, out_lo = sb("qk_out_hi", [P, 2, CH], F32R), sb("qk_out_lo", [P, 2, CH], F32R)
        v_out = sb("v_out", [P, 2, E], F32)
        ident = sb("ident1", [P, P], F32)
        ones = sb("ones1", [P, P], F32)
        bq_c = sb("bq_c", [P, CT], F32)
        bk_c = sb("bk_c", [P, 2], F32)
        bks_c = sb("bks_c", [P, 2], F32)
        bv_r = sb("bv_r", [P, E], F32)
        absum = sb("absum", [P, NCH], F32)
        bsum = sb("bsum", [P, B], F32)
        tr = [st.enter_context(nc.psum_tensor(f"tr{i}", [P, CH], F32)) for i in range(2)]
        pq = [st.enter_context(nc.psum_tensor(f"pq{i}", [P, CH], F32)) for i in range(4)]
        pkv = [st.enter_context(nc.psum_tensor(f"pkv{i}", [P, CH], F32)) for i in range(2)]

        x_loaded, c_loaded, m_loaded = sem("x_loaded"), sem("c_loaded"), sem("m_loaded")
        w_loaded = [sem(f"w_loaded{i}") for i in range(3)]
        consts_loaded = sem("consts_loaded")
        w_hi, w_lo = sem("w_hi"), sem("w_lo")
        tr_ready, tr_hi, tr_lo = sem("tr_ready"), sem("tr_hi"), sem("tr_lo")
        out_ready, hi_done, out_done = sem("out_ready"), sem("hi_done"), sem("out_done")
        qk_stored = [sem(f"qk_stored{i}") for i in range(2)]
        v_stored = [sem(f"v_stored{i}") for i in range(2)]
        mask_summed, small_done, flag_ready = sem("mask_summed"), sem("small_done"), sem("flag_ready")
        ones_set = sem("ones_set")

        T, OUT, QK, V = 2 * CT, 14, 10, 4
        tr_ctx = lambda i, k: CT + T * i + k
        tr_x = lambda i, k: T * i + k

        def steps(last):
            for m in range(CT):
                yield "tc", m
                yield "q", m
            x_at = [(0, 1), (2, 3), (4,), (5,), (6,), (7,)]
            for n in range(6):
                yield ("k", n) if n < 2 else ("v", n - 2)
                if not last:
                    for k in x_at[n]:
                        yield "tx", k

        def iterations(engine, body):
            body(0, False)
            with engine.Fori(1, NCH - 1) as i:
                body(i, False)
            body(NCH - 1, True)

        block = st.enter_context(nc.Block())

        @block.sync
        def _(sp):
            sp.dma_start(ident[:], ident_dram).then_inc(consts_loaded, 16)
            sp.dma_start(x_tok[:], x_v[0]).then_inc(x_loaded, 16)
            sp.dma_start(c_tok[:], wq_v[:, 0:4, :]).then_inc(w_loaded[0], 16)
            sp.dma_start(m_tok[:], wq_v[:, 4:8, :]).then_inc(w_loaded[1], 16)
            sp.dma_start(bq_c[:], bq.rearrange("(m p) -> p m", p=P), allow_slow_non_contiguous=True).then_inc(consts_loaded, 16)
            sp.dma_start(bk_c[:], bk.rearrange("(m p) -> p m", p=P), allow_slow_non_contiguous=True).then_inc(consts_loaded, 16)
            sp.dma_start(bv_r[:], bv.partition_broadcast(P)).then_inc(consts_loaded, 16)
            sp.wait_ge(tr_ready, CT)
            wkv = x_tok[:].rearrange("p t c -> p (t c)").rearrange("p (w k e) -> p w k e", w=2, e=E)
            sp.dma_start(wkv[:, 0], wk_v).then_inc(w_loaded[2], 16)
            sp.dma_start(wkv[:, 1], wv_v).then_inc(w_loaded[2], 16)
            sp.wait_ge(w_lo, 4)
            sp.dma_start(c_tok[:], c_v[0]).then_inc(c_loaded, 16)
            sp.wait_ge(w_lo, 8)
            sp.dma_start(m_tok[:], m_v[0]).then_inc(m_loaded, 16)
            sp.wait_ge(w_lo, 10)

            def body(i, last):
                if not last:
                    wait(sp, tr_ready, tr_x(i, CT))
                    sp.dma_start(x_tok[:], x_v[bass.ds(i + 1, 1)].rearrange("o p t c -> (o p) t c")).then_inc(x_loaded, 16)
                for what, n in steps(last):
                    if what in "qk":
                        j = n if what == "q" else CT + n
                        wait(sp, out_done, OUT * i + j + 1)
                        hi, lo = (q_hi_v, q_lo_v) if what == "q" else (k_hi_v, k_lo_v)
                        for part, dram in ((out_hi, hi), (out_lo, lo)):
                            to = dram[bass.ds(i, 1), n] if what == "q" else dram[bass.ds(i, 1), n * P:(n + 1) * P]
                            sp.dma_start(to.rearrange("o p l -> (o p) l"), f32(part[:, j % 2])).then_inc(qk_stored[j % 2], 16)
                    if what == "v":
                        wait(sp, out_done, OUT * i + QK + n + 1)
                        sp.dma_start(v_v[bass.ds(i, 1), n].rearrange("o p e -> (o p) e"), v_out[:, n % 2]).then_inc(v_stored[n % 2], 16)
                    if what == "q" and n == CT - 1 and not last:
                        wait(sp, tr_ready, tr_ctx(i, CT))
                        sp.dma_start(c_tok[:], c_v[bass.ds(i + 1, 1)].rearrange("o p t c -> (o p) t c")).then_inc(c_loaded, 16)
                    if what == "k" and n == 0 and not last:
                        wait(sp, mask_summed, i + 1)
                        sp.dma_start(m_tok[:], m_v[bass.ds(i + 1, 1)].rearrange("o p t c -> (o p) t c")).then_inc(m_loaded, 16)
            iterations(sp, body)
            for r in range(2):
                sp.wait_ge(qk_stored[r], NCH * QK // 2 * 32)
                sp.wait_ge(v_stored[r], NCH * V // 2 * 16)

        @block.tensor
        def _(pe):
            def transpose_tile(tok, at, k):
                wait(pe, tr_lo, at - 1)
                for t in range(TT):
                    last = nc.tensor.transpose(tr[k % 2][:, t * P:(t + 1) * P], tok[:, t, k * P:(k + 1) * P], ident[:])
                last.then_inc(tr_ready, 1)

            def product(bank, terms):
                for n, (a, b) in enumerate(terms):
                    last = nc.tensor.matmul(bank, a, b, start=n == 0, stop=n == len(terms) - 1)
                last.then_inc(out_ready, 1)

            pe.wait_ge(consts_loaded, 64)
            pe.wait_ge(x_loaded, 16)
            for k in range(CT):
                transpose_tile(x_tok, k, k)

            def body(i, last):
                for what, n in steps(last):
                    if what == "tc":
                        if n == 0:
                            wait(pe, c_loaded, 16 * (i + 1))
                        transpose_tile(c_tok, tr_ctx(i, n), n)
                    if what == "tx":
                        if n == 0:
                            wait(pe, x_loaded, 16 * (i + 2))
                        transpose_tile(x_tok, tr_x(i + 1, n), n)
                    if what == "q":
                        if n == 0:
                            wait(pe, tr_lo, tr_x(i, CT))
                            if isinstance(i, int):
                                wait(pe, w_lo, 8)
                        wait(pe, out_done, OUT * i + n - 3 if n >= 4 else OUT * (i - 1) + n + 5)
                        cols = slice(n * P, (n + 1) * P)
                        product(pq[n % 4][:], [(w[:, k, cols], t[:, k]) for k in range(CT)
                                               for w, t in ((wq_hi, xT_hi), (wq_lo, xT_hi), (wq_hi, xT_lo))])
                    if what == "k":
                        if n == 0:
                            wait(pe, tr_lo, tr_ctx(i, CT))
                            if isinstance(i, int):
                                wait(pe, w_lo, 10)
                        wait(pe, out_done, OUT * i + n - 1)
                        cols = slice(n * P, (n + 1) * P)
                        product(pkv[n % 2][:], [(w[:, k, cols], t[:, k]) for k in range(CT)
                                                for w, t in ((wk_hi, cT_hi), (wk_lo, cT_hi), (wk_hi, cT_lo))])
                    if what == "v":
                        wait(pe, out_done, OUT * i + CT + n + 1)
                        cols = slice(n * P, (n + 1) * P)
                        product(pkv[n % 2][:, 0:E], [(t[:, k, cols], w[:, k]) for k in range(CT)
                                                     for w, t in ((wv_hi, cT_hi), (wv_lo, cT_hi), (wv_hi, cT_lo))])
            iterations(pe, body)
            pe.wait_ge(ones_set, 1)
            pe.wait_ge(mask_summed, NCH)
            nc.tensor.matmul(tr[0][:, 0:NCH], ones[:], absum[:], start=True, stop=True).then_inc(flag_ready, 1)

        @block.scalar
        def _(act):
            def transposed(at, k, hi):
                wait(act, tr_ready, at + 1)
                nc.scalar.activation(hi[:, k], tr[k % 2][:], ACT.Copy).then_inc(tr_hi, 1)

            act.wait_ge(x_loaded, 16)
            for k in range(CT):
                transposed(k, k, xT_hi)
            for k in range(CT):
                src = (c_tok, m_tok)[k // 4]
                act.wait_ge(w_loaded[k // 4], 16)
                nc.scalar.activation(wq_hi[:, k], src[:, k % 4], ACT.Copy).then_inc(w_hi, 1)
            wkv = x_tok[:].rearrange("p t c -> p (t c)").rearrange("p (w k e) -> p w k e", w=2, e=E)
            act.wait_ge(w_loaded[2], 32)
            nc.scalar.activation(wk_hi[:], wkv[:, 0], ACT.Copy, scale=SCALE).then_inc(w_hi, 1)
            nc.scalar.activation(wv_hi[:], wkv[:, 1], ACT.Copy).then_inc(w_hi, 1)
            act.wait_ge(small_done, 1)

            def body(i, last):
                for what, n in steps(last):
                    if what == "tc":
                        if n == 0:
                            wait(act, out_ready, OUT * i)
                        transposed(tr_ctx(i, n), n, cT_hi)
                    if what == "tx":
                        if n == 0:
                            wait(act, out_ready, OUT * i + CT)
                        transposed(tr_x(i + 1, n), n, xT_hi)
                    if what in "qk":
                        j = n if what == "q" else CT + n
                        bank, bias = (pq[n % 4], bq_c) if what == "q" else (pkv[n % 2], bks_c)
                        wait(act, out_ready, OUT * i + j + 1)
                        wait(act, qk_stored[j % 2], 32 * (QK // 2 * i + j // 2))
                        nc.scalar.activation(out_hi[:, j % 2], bank[:], ACT.Identity, bias=bias[:, n:n + 1]).then_inc(hi_done, 1)
            iterations(act, body)

        @block.vector
        def _(dve):
            def transposed(at, k, hi, lo):
                wait(dve, tr_hi, at + 1)
                nc.vector.tensor_tensor(lo[:, k], tr[k % 2][:], f32(hi[:, k]), ALU.subtract).then_inc(tr_lo, 1)

            nc.vector.memset(ones[:], 1.0).then_inc(ones_set, 1)
            for k in range(CT):
                transposed(k, k, xT_hi, xT_lo)
            for k in range(CT):
                src = (c_tok, m_tok)[k // 4]
                dve.wait_ge(w_hi, k + 1)
                nc.vector.tensor_tensor(wq_lo[:, k], src[:, k % 4], f32(wq_hi[:, k]), ALU.subtract).then_inc(w_lo, 1)
            wkv = x_tok[:].rearrange("p t c -> p (t c)").rearrange("p (w k e) -> p w (k e)", w=2, e=E)
            flat = lambda t: f32(t[:]).rearrange("p k e -> p (k e)")
            dve.wait_ge(w_hi, CT + 1)
            nc.vector.scalar_tensor_tensor(wk_lo[:].rearrange("p k e -> p (k e)"), wkv[:, 0], SCALE, flat(wk_hi),
                                           ALU.mult, ALU.subtract).then_inc(w_lo, 1)
            dve.wait_ge(w_hi, CT + 2)
            nc.vector.tensor_tensor(wv_lo[:].rearrange("p k e -> p (k e)"), wkv[:, 1], flat(wv_hi), ALU.subtract).then_inc(w_lo, 1)
            dve.wait_ge(consts_loaded, 64)
            nc.vector.tensor_scalar(bks_c[:], bk_c[:], SCALE, None, ALU.mult).then_inc(small_done, 1)
            dve.wait_ge(small_done, 1)

            def body(i, last):
                for what, n in steps(last):
                    if what == "tc":
                        transposed(tr_ctx(i, n), n, cT_hi, cT_lo)
                    if what == "tx":
                        transposed(tr_x(i + 1, n), n, xT_hi, xT_lo)
                    if what in "qk":
                        j = n if what == "q" else CT + n
                        bank, bias = (pq[n % 4], bq_c) if what == "q" else (pkv[n % 2], bks_c)
                        wait(dve, hi_done, QK * i + j + 1)
                        nc.vector.scalar_tensor_tensor(out_lo[:, j % 2], bank[:], bias[:, n:n + 1], f32(out_hi[:, j % 2]),
                                                       ALU.add, ALU.subtract).then_inc(out_done, 1)
                    if what == "v":
                        wait(dve, out_ready, OUT * i + QK + n + 1)
                        wait(dve, v_stored[n % 2], 16 * (V // 2 * i + n // 2))
                        nc.vector.tensor_tensor(v_out[:, n % 2], pkv[n % 2][:, 0:E], bv_r[:], ALU.add).then_inc(out_done, 1)
                    if what == "q" and n == CT - 1:
                        wait(dve, m_loaded, 16 * (i + 1))
                        nc.vector.tensor_reduce(absum[:, bass.ds(i, 1)], m_tok[:].rearrange("p t s -> p (t s)"), AX.X, ALU.add,
                                                apply_absolute_value=True).then_inc(mask_summed, 1)
            iterations(dve, body)
            dve.wait_ge(flag_ready, 1)
            halves = tr[0][:, 0:NCH].rearrange("p (b h) -> p b h", h=HALVES)
            nc.vector.tensor_reduce(bsum[:], halves, AX.X, ALU.add).then_inc(small_done, 1)
            dve.wait_ge(small_done, 2)
            per_batch = PAIRS // B
            nc.vector.tensor_scalar(flags[:].rearrange("p (b r) -> p b r", r=per_batch),
                                    bsum[:].unsqueeze(2).to_broadcast([P, B, per_batch]),
                                    0.0, None, ALU.not_equal).then_inc(small_done, 1)
            dve.wait_ge(small_done, 3)



def attend(nc, mask, ident_dram, scratch, flags):
    q_hi_v = scratch["q_hi"].rearrange("i g (h d) l -> i g d h l", d=D)
    q_lo_v = scratch["q_lo"].rearrange("i g (h d) l -> i g d h l", d=D)
    k_v = {part: scratch[part].rearrange("(b f) e s -> b e f s", f=HALVES) for part in ("k_hi", "k_lo")}
    v_v = scratch["v"].rearrange("(b t p) e -> b p t e", t=ST, p=P)
    o_v = scratch["o"]
    mask_v = mask.rearrange("b o (t p) s -> t (b o) p s", p=P)
    R3 = 3 * D
    R = R3 + 2
    NX = NG * HALVES
    QT = ST // HALVES
    ROWS = QT * HEADS
    PER_STEP = ROWS // ST
    ADDS = 5
    SETS = ST - ADDS

    LEAD = 6
    LAST_ROWS = (ROWS - LEAD) // PER_STEP - 1
    SUMS_AT, NORM_AT, TURN_AT = 1, SETS + 1, LAST_ROWS + 2

    with ExitStack() as st:
        sb = lambda name, shape, dt: st.enter_context(nc.sbuf_tensor(name, shape, dt))
        ps = lambda name, shape: st.enter_context(nc.psum_tensor(name, shape, F32))
        sem = lambda name: st.enter_context(nc.semaphore(name))
        q_st = [sb(f"q_st{i}", [P, HEADS, CH], F32R) for i in range(4)]
        k_max = [sb(f"k_max{u}", [P, L], F32R) for u in range(2)]
        k_exp = [sb(f"k_exp{u}", [P, L], F32R) for u in range(2)]
        v_sb = [sb(f"v_sb{u}", [P, ST, D], F32) for u in range(2)]
        mask_q = sb("mask_q", [P, ST, L], F32)
        mask_k = sb("mask_k", [P, ST, L], F32)
        probs = sb("probs", [P, ST, HEADS, CH], F32)
        key_sum = [sb(f"key_sum{f}", [P, HEADS * CH], F32) for f in range(HALVES)]
        sums_t, recip_row = sb("sums_t", [P, CH], F32), sb("recip_row", [P, CH // D], F32)
        recip, o_raw, o_n = sb("recip", [P, CH], F32), sb("o_raw", [P, CH], F32), sb("o_n", [P, CH], F32)
        junk = sb("junk", [P, 2, L], BF16)
        row_max = sb("row_max", [P, HALVES, ROWS], F32)
        neg_max = sb("neg_max", [P, P // ROWS, ROWS], F32R)
        neg_max_t = sb("neg_max_t", [2 * ROWS, P], F32)
        ones = sb("ones2", [P, D], F32)
        ident = sb("ident2", [P, P], F32)
        sc_q = [ps(f"sc_q{i}", [P, L]) for i in range(2)]
        sc_k = [ps(f"sc_k{i}", [P, CH]) for i in range(2)]
        out_ps = ps("out_ps", [P, CH])
        misc = ps("misc", [P, CH])

        consts_loaded, consts_set = sem("consts2_loaded"), sem("consts2_set")
        mask_loaded = [sem(f"mask_loaded{t}") for t in range(ST)]
        q_loaded = [sem(f"q_loaded{i}") for i in range(4)]
        km_loaded = [sem(f"km_loaded{u}") for u in range(2)]
        kv_loaded = [sem(f"kv_loaded{u}") for u in range(2)]
        nm_loaded = [sem(f"nm_loaded{i}") for i in range(4)]
        q_scored, q_maxed, seen = sem("q_scored"), sem("q_maxed"), sem("seen2")
        k_scored, k_masked, exp_done = sem("k_scored"), sem("k_masked"), sem("exp_done")
        pv_done, key_added = sem("pv_done"), sem("key_added")
        sums_done, raw_out, sums_read, out_ready = sem("sums_done"), sem("raw_out"), sem("sums_read"), sem("o_ready")
        max_split, max_turned, max_ready, o_stored = sem("max_split"), sem("max_turned"), sem("max_ready"), sem("o_stored")
        mk_turned, mk_ready = sem("mk_turned"), sem("mk_ready")
        chain, norm = sem("max_chain"), sem("norm_chain")

        EXPS = HEADS * ST

        def place(it, j):
            return 4 * it + j, j % 4, it + j // 4

        def ahead(it, j, s):
            at = [LEAD + PER_STEP * s + r for r in range(PER_STEP)]
            rows = [(1 + a // ROWS, a % ROWS) for a in at]
            return [(d, r) for d, r in rows if not isinstance(it, int) or 4 * it + j + d < NX]

        def follows(it, j):
            return not isinstance(it, int) or 4 * it + j + 1 < NX

        def fours(engine, body):
            body(0)
            with engine.Fori(1, NX // 4 - 1) as it:
                body(it)
            body(NX // 4 - 1)

        block = st.enter_context(nc.Block())

        @block.sync
        def _(sp):
            def load_mask(t, b):
                sp.dma_start(mask_q[:, t], mask_v[t, bass.ds(b, 1)].rearrange("o p s -> (o p) s")).then_inc(mask_loaded[t], 16)

            def load_q(it, j):
                x, i, _ = place(it, j)
                b, g = x // (HALVES * KVH), x // HALVES % KVH
                for row, part in ((0, q_hi_v), (1, q_hi_v), (2, q_lo_v)):
                    src = part[bass.ds(b * HALVES + j % HALVES, 1), bass.ds(g, 1)].rearrange("o r d h l -> (o r d) h l")
                    sp.dma_start(f32(q_st[i][row * D:(row + 1) * D]), src).then_inc(q_loaded[i], 16)

            def load_k(n, dst, semaphore):
                b, g = n // KVH, n % KVH
                for row, part in ((0, "k_hi"), (1, "k_lo"), (2, "k_hi")):
                    src = k_v[part][bass.ds(b, 1), bass.ds(g * D, D)].rearrange("o d f s -> (o d) f s")
                    sp.dma_start(f32(dst[row * D:(row + 1) * D]).rearrange("d (f s) -> d f s", f=HALVES), src).then_inc(semaphore, 16)

            def load_v(n, u):
                b, g = n // KVH, n % KVH
                src = v_v[bass.ds(b, 1), :, :, bass.ds(g * D, D)].rearrange("o p t e -> (o p) t e")
                sp.dma_start(v_sb[u][:], src).then_inc(kv_loaded[u], 16)

            def store_o(it, j):
                x, _, _ = place(it, j)
                wait(sp, out_ready, x + 1)
                b, g = x // (HALVES * KVH), x // HALVES % KVH
                dst = o_v[bass.ds(b * HALVES + j % HALVES, 1), bass.ds(g, 1)].rearrange("o r p l -> (o r p) l")
                sp.dma_start(dst, o_n[:]).then_inc(o_stored, 16)

            def store_max(it, j):
                x, i, _ = place(it, j)
                wait(sp, max_ready, x + 1)
                for part in range(2):
                    sp.dma_start(f32(q_st[i][R3 + part:R3 + part + 1]).rearrange("o h (t l) -> o (h t) l", l=P),
                                 neg_max_t[part * ROWS:(part + 1) * ROWS]).then_inc(nm_loaded[i], 16)

            load_q(0, 0)
            load_k(0, k_max[0], km_loaded[0])
            load_mask(0, 0)
            sp.dma_start(ident[:], ident_dram).then_inc(consts_loaded, 16)
            for t in range(1, QT):
                load_mask(t, 0)
            load_q(0, 1)
            load_k(0, k_exp[0], kv_loaded[0])
            load_v(0, 0)
            for t in range(QT, ST):
                load_mask(t, 0)
            load_q(0, 2)
            load_k(1, k_max[1], km_loaded[1])
            store_max(0, 0)

            def body(it):
                first, last = isinstance(it, int) and it == 0, isinstance(it, int) and it > 0
                for j in range(4):
                    x, _, _ = place(it, j)
                    u, f = divmod(j, 2)
                    n = 2 * it + u
                    if not (last and j > 0):
                        wait(sp, k_scored, EXPS * x)
                        load_q(it, j + 3)
                    if f == 0 and not (last and u == 1):
                        load_k(n + 1, k_exp[1 - u], kv_loaded[1 - u])
                        wait(sp, pv_done, ST * x)
                        load_v(n + 1, 1 - u)
                    if not (first and j == 0):
                        store_o(it, j - 1)
                    if not (last and j == 3):
                        store_max(it, j + 1)
                    if f == 0 and not last:
                        wait(sp, q_maxed, ROWS * (x + 2))
                        load_k(n + 2, k_max[u], km_loaded[u])
                    if j in (1, 2) and not first and not last:
                        with sp.If((it % (PAIRS // B)) == PAIRS // B - 1):
                            wait(sp, q_maxed, ROWS * (x + 2))
                            for t in range(QT):
                                load_mask(QT * (j - 1) + t, (it + 1) // (PAIRS // B))
            fours(sp, body)
            store_o(NX // 4 - 1, 3)
            sp.wait_ge(o_stored, 16 * NX)

        @block.gpsimd
        def _(pool):
            def body(it):
                for j in range(4):
                    x, _, _ = place(it, j)
                    total = key_sum[j % 2][:]
                    flat = lambda t: probs[:, t].rearrange("p h l -> p (h l)")
                    for k in range(ADDS):
                        wait(pool, exp_done, EXPS * x + HEADS * (k + 2))
                        if k == 0:
                            wait(pool, sums_done, x - 1)
                        else:
                            wait(pool, key_added, ADDS * x + k)
                        nc.gpsimd.tensor_tensor(total, flat(0) if k == 0 else total, flat(k + 1), ALU.add).then_inc(key_added, 1)
            fours(pool, body)

        @block.tensor
        def _(pe):
            def score_q(it, j, r):
                x, i, turn = place(it, j)
                t, h = divmod(r, HEADS)
                if r == 0:
                    wait(pe, q_loaded[i], 48 * (turn + 1))
                    if i % 2 == 0:
                        wait(pe, km_loaded[i // 2], 48 * (turn + 1))
                wait(pe, q_maxed, ROWS * x + r - 1)
                for f in range(HALVES):
                    last = nc.tensor.matmul(sc_q[r % 2][:, f * CH:(f + 1) * CH], q_st[i][0:R3, h, t * P:(t + 1) * P],
                                            k_max[i // 2][0:R3, f * CH:(f + 1) * CH], start=True, stop=True)
                last.then_inc(q_scored, 1)

            def turn_max(x):
                wait(pe, max_split, x + 1)
                wait(pe, sums_read, x - 1)
                nc.tensor.transpose(misc[:, 0:P], f32(neg_max[:]).rearrange("p a c -> p (a c)"), ident[:]).then_inc(max_turned, 1)

            def score_k(it, j, s, h):
                x, i, _ = place(it, j)
                wait(pe, exp_done, EXPS * x + HEADS * s + h - 1)
                nc.tensor.matmul(sc_k[h % 2][:], k_exp[i // 2][0:R, s * P:(s + 1) * P], q_st[i][0:R, h],
                                 start=True, stop=True).then_inc(k_scored, 1)

            def times_v(it, j, s):
                x, i, _ = place(it, j)
                wait(pe, exp_done, EXPS * x + HEADS * (s + 1))
                if s == 0:
                    wait(pe, raw_out, x)
                for h in range(HEADS):
                    last = nc.tensor.matmul(out_ps[h * D:(h + 1) * D], v_sb[i // 2][:, s], probs[:, s, h],
                                            start=s == 0, stop=s == ST - 1, tile_position=(0, h * D))
                last.then_inc(pv_done, 1)

            def sum_keys(x, f, part):
                if part == 0 and not (isinstance(x, int) and x == NX - 1):
                    wait(pe, max_ready, x + 2)
                if part == SETS - 1:
                    wait(pe, key_added, ADDS * (x + 1))
                for h in range(HEADS):
                    src = probs[:, ADDS + 1 + part, h] if part < SETS - 1 else key_sum[f][:, h * CH:(h + 1) * CH]
                    last = nc.tensor.matmul(misc[h * D:(h + 1) * D], ones[:], src, start=part == 0,
                                            stop=part == SETS - 1, tile_position=(0, h * D))
                if part == SETS - 1:
                    last.then_inc(sums_done, 1)

            def turn_mask(it):
                for t in range(ST):
                    wait(pe, mask_loaded[t], 16 * (it // (PAIRS // B) + 1))
                for m in range(2 * ST):
                    t, f = divmod(m, 2)
                    wait(pe, mk_ready, 2 * ST * it + m)
                    for r in range(4):
                        last = nc.tensor.transpose(misc[:, r * P:(r + 1) * P], mask_q[:, 4 * f + r, t * P:(t + 1) * P], ident[:])
                    last.then_inc(mk_turned, 1)

            pe.wait_ge(consts_loaded, 16)
            pe.wait_ge(consts_set, 4)
            for a in range(ROWS + LEAD):
                score_q(0, a // ROWS, a % ROWS)
                if a == ROWS:
                    turn_max(0)

            def body(it):
                first = isinstance(it, int) and it == 0
                has_mask = pe.value_load(flags[0:1, bass.ds(it, 1)], min_val=0, max_val=1)
                with pe.If(has_mask != 0):
                    wait(pe, sums_read, 4 * it - 1)
                    wait(pe, max_ready, 4 * it + 1)
                    turn_mask(it)
                with pe.Else():
                    wait(pe, mk_turned, 2 * ST * it)
                    pe.sem_inc(mk_turned, 2 * ST)
                for j in range(4):
                    x, i, turn = place(it, j)
                    for s in range(ST):
                        if s == 0:
                            if j % 2 == 0:
                                wait(pe, kv_loaded[i // 2], 64 * (turn + 1))
                            wait(pe, nm_loaded[i], 32 * (turn + 1))
                        rows = ahead(it, j, s)
                        if s == TURN_AT and follows(it, j):
                            turn_max(x + 1)
                        score_k(it, j, s, 0)
                        for d, r in rows[:1]:
                            score_q(it, j + d, r)
                        score_k(it, j, s, 1)
                        if s > 0:
                            times_v(it, j, s - 1)
                        elif not (first and j == 0):
                            times_v(it, j - 1, ST - 1)
                        score_k(it, j, s, 2)
                        for d, r in rows[1:]:
                            score_q(it, j + d, r)
                        score_k(it, j, s, 3)
                        if SUMS_AT <= s < SUMS_AT + SETS and not (first and j == 0):
                            sum_keys(x - 1, (j - 1) % 2, s - SUMS_AT)
            fours(pe, body)
            times_v(NX // 4 - 1, 3, ST - 1)
            wait(pe, sums_read, NX - 1)
            for part in range(SETS):
                sum_keys(NX - 1, 1, part)

        @block.scalar
        def _(act):
            def exponentials(it, j, s, h, masked):
                x, _, _ = place(it, j)
                if h == 0 and not (isinstance(it, int) and it == 0 and j == 0):
                    wait(act, pv_done, ST * (x - 1) + s + 1)
                    if s <= ADDS:
                        wait(act, key_added, ADDS * (x - 1) + max(s, 1))
                    elif s == ADDS + 1:
                        wait(act, sums_done, x)
                wait(act, k_masked if masked else k_scored, EXPS * x + HEADS * s + h + 1)
                nc.scalar.activation(probs[:, s, h], sc_k[h % 2][:], ACT.Exp).then_inc(exp_done, 1)

            def read_out(x):
                wait(act, pv_done, ST * (x + 1))
                wait(act, out_ready, x)
                nc.scalar.activation(o_raw[:], out_ps[:], ACT.Copy).then_inc(raw_out, 1)

            def read_max(it, j):
                x, i, turn = place(it, j)
                wait(act, max_turned, x + 1)
                if not (isinstance(it, int) and 4 * it + j == 0):
                    wait(act, nm_loaded[(j - 1) % 4], 32 * (it + (j - 1) // 4 + 1))
                nc.scalar.activation(neg_max_t[:], misc[0:2 * ROWS, 0:P], ACT.Copy).then_inc(max_ready, 1)

            read_max(0, 0)

            def halves(it, masked):
                first = isinstance(it, int) and it == 0
                for j in range(4):
                    x, _, _ = place(it, j)
                    for s in range(ST):
                        for h in range(HEADS):
                            exponentials(it, j, s, h, masked)
                            if s == 0 and h == 2 and not (first and j == 0):
                                read_out(x - 1)
                            if s == TURN_AT and h == 0 and follows(it, j):
                                read_max(it, j + 1)

            def body(it):
                has_mask = act.value_load(flags[0:1, bass.ds(it, 1)], min_val=0, max_val=1)
                with act.If(has_mask != 0):
                    wait(act, k_masked, 4 * EXPS * it)
                    for m in range(2 * ST):
                        t, f = divmod(m, 2)
                        wait(act, mk_turned, 2 * ST * it + m + 1)
                        nc.scalar.activation(mask_k[:, t, f * CH:(f + 1) * CH], misc[:], ACT.Copy).then_inc(mk_ready, 1)
                    halves(it, True)
                with act.Else():
                    wait(act, mk_ready, 2 * ST * it)
                    act.sem_inc(mk_ready, 2 * ST)
                    halves(it, False)
            fours(act, body)
            read_out(NX - 1)

        @block.vector
        def _(dve):
            nc.vector.memset(ones[:], 1.0).then_inc(consts_set, 1)
            nc.vector.memset(f32(neg_max[:, 2:]), 0.0).then_inc(consts_set, 1)
            for u in range(2):
                nc.vector.memset(f32(k_exp[u][R3:R]), 1.0).then_inc(consts_set, 1)

            def maximum(it, j, r):
                x, i, turn = place(it, j)
                t, h = divmod(r, HEADS)
                tile = j % 2 * QT + t
                if h == 0:
                    wait(dve, mask_loaded[tile], 16 * (turn // (PAIRS // B) + 1))
                wait_before(dve, q_scored, ROWS * x + r + 1, seen)
                nc.vector.tensor_tensor_reduce(out=junk[:, r % 2], in0=sc_q[r % 2][:], in1=mask_q[:, tile],
                                               scale=1.0, scalar=LOWEST, op0=ALU.add, op1=ALU.max,
                                               accum_out=row_max[:, j % 2, h * QT + t:h * QT + t + 1]).then_inc(q_maxed, 1)

            def split_max(x, f):
                wait(dve, q_maxed, ROWS * (x + 1))
                wait(dve, max_turned, x)
                nc.vector.tensor_scalar(neg_max[:, 0], row_max[:, f], -1.0, None, ALU.mult).then_inc(chain, 1)
                wait(dve, chain, x + 1)
                nc.vector.scalar_tensor_tensor(neg_max[:, 1], row_max[:, f], -1.0, f32(neg_max[:, 0]), ALU.mult,
                                               ALU.subtract).then_inc(max_split, 1)

            def normalize(x):
                wait(dve, sums_done, x + 1)
                nc.vector.transpose(sums_t[:], misc[:]).then_inc(sums_read, 1)
                wait(dve, sums_read, x + 1)
                nc.vector.reciprocal(recip_row[:], sums_t[:].rearrange("p (j c) -> p j c", c=D)[:, :, 0]).then_inc(norm, 1)
                wait(dve, norm, 2 * x + 1)
                nc.vector.transpose(recip[:], recip_row[:].unsqueeze(2).to_broadcast([P, CH // D, D])).then_inc(norm, 1)
                wait(dve, norm, 2 * x + 2)
                wait(dve, raw_out, x + 1)
                wait(dve, o_stored, 16 * x)
                nc.vector.tensor_tensor(o_n[:], o_raw[:], recip[:], ALU.mult).then_inc(out_ready, 1)

            def add_mask(x, j, s, h):
                wait(dve, k_scored, EXPS * x + HEADS * s + h + 1)
                m = mask_k[:, s, j % 2 * CH:(j % 2 + 1) * CH]
                nc.vector.tensor_tensor(sc_k[h % 2][:], sc_k[h % 2][:], m, ALU.add).then_inc(k_masked, 1)

            for a in range(ROWS + LEAD):
                maximum(0, a // ROWS, a % ROWS)
                if a == ROWS - 1:
                    split_max(0, 0)

            def halves(it, masked):
                first = isinstance(it, int) and it == 0
                for j in range(4):
                    x, _, _ = place(it, j)
                    for s in range(ST):
                        rows = ahead(it, j, s)
                        for h in range(HEADS):
                            if masked:
                                add_mask(x, j, s, h)
                            for d, r in rows[h // 2:h // 2 + 1] if h % 2 == 0 else []:
                                maximum(it, j + d, r)
                                if r == ROWS - 1:
                                    split_max(x + d, (j + d) % 2)
                            if s == NORM_AT and h == 0 and not (first and j == 0):
                                normalize(x - 1)

            def body(it):
                has_mask = dve.value_load(flags[0:1, bass.ds(it, 1)], min_val=0, max_val=1)
                with dve.If(has_mask != 0):
                    wait(dve, mk_ready, 2 * ST * (it + 1))
                    halves(it, True)
                with dve.Else():
                    wait(dve, k_masked, 4 * EXPS * it)
                    dve.sem_inc(k_masked, 4 * EXPS)
                    halves(it, False)
            fours(dve, body)
            normalize(NX - 1)



def project_out(nc, x, wo, bo, gamma, beta, scratch, out):
    o_v = scratch["o"].rearrange("i g p l -> i p g l")
    x_v = x.rearrange("b (n t p) c -> (b n) p t c", t=TT, p=P)
    out_v = out.rearrange("b (n t p) c -> (b n) t p c", t=TT, p=P)
    wo_v = wo.rearrange("(k p) n -> p k n", p=P)
    STATS = nc.vector.BN_STATS_DIM
    NC = H // CH

    with ExitStack() as st:
        sb = lambda name, shape, dt: st.enter_context(nc.sbuf_tensor(name, shape, dt))
        sem = lambda name: st.enter_context(nc.semaphore(name))
        o_in = sb("o_in", [P, CT, CH], F32)
        oT_hi = [sb(f"oT_hi{i}", [P, CT, CH], F32R) for i in range(2)]
        oT_lo = [sb(f"oT_lo{i}", [P, CT, CH], F32R) for i in range(2)]
        x_res = [sb(f"x_res{i}", [P, TT, H], F32) for i in range(2)]
        wo_hi, wo_lo = sb("wo_hi", [P, CT, H], F32R), sb("wo_lo", [P, CT, H], F32R)
        bo_row, bo_hi, bo_lo = sb("bo_row", [1, H], F32), sb("bo_hi", [1, H], F32R), sb("bo_lo", [1, H], F32R)
        bo_two = sb("bo_two", [2, H], F32R)
        ones_f = sb("ones3f", [2, P], F32)
        ones = sb("ones3", [2, P], F32R)
        gamma_r, beta_r = sb("gamma_r", [P, H], F32), sb("beta_r", [P, H], F32)
        y, z = sb("y", [P, 2, H], F32), sb("z", [P, 2, H], F32)
        stats, mv = sb("stats", [P, NC, STATS], F32), sb("mv", [P, 2, 2], F32)
        std, rstd, shift = sb("std", [P, 2], F32), sb("rstd", [P, 2], F32), sb("shift", [P, 2], F32)
        eps = sb("eps", [P, 1], F32)
        acc = [st.enter_context(nc.psum_tensor(f"acc{i}", [P, H], F32)) for i in range(2)]

        w_loaded = [sem(f"wo_loaded{i}") for i in range(2)]
        o_loaded, bo_loaded, affine_loaded = sem("o_loaded"), sem("bo_loaded"), sem("affine_loaded")
        x_loaded = [sem(f"xr_loaded{i}") for i in range(2)]
        w_hi, w_lo, bo_split, bo_ready = sem("wo_hi_done"), sem("wo_lo_done"), sem("bo_split"), sem("bo_ready")
        ones_set, consts_set = sem("ones3_set"), sem("consts3_set")
        o_hi, o_lo = sem("o_hi"), sem("o_lo")
        projected, summed, measured, rooted = sem("projected"), sem("summed"), sem("measured"), sem("rooted")
        inverted, centred, scaled, done = sem("inverted"), sem("centred"), sem("scaled"), sem("done")
        statted, weighed, seen = sem("statted"), sem("weighed"), sem("seen3")
        stored = [sem(f"stored{i}") for i in range(2)]
        Q, QK = 4, CT // 4

        block = st.enter_context(nc.Block())

        @block.sync
        def _(sp):
            def load_o(c):
                sp.dma_start(o_in[:], o_v[bass.ds(c, 1)].rearrange("o p g l -> (o p) g l")).then_inc(o_loaded, 16)

            def load_x(c, r):
                sp.dma_start(x_res[r][:], x_v[bass.ds(c, 1)].rearrange("o p t c -> (o p) t c")).then_inc(x_loaded[r], 16)

            sp.dma_start(bo_row[:], bo.rearrange("(o n) -> o n", o=1)).then_inc(bo_loaded, 16)
            for i in range(2):
                sp.dma_start(x_res[i][:], wo_v[:, 4 * i:4 * i + 4, :]).then_inc(w_loaded[i], 16)
            load_o(0)
            sp.dma_start(gamma_r[:], gamma.partition_broadcast(P)).then_inc(affine_loaded, 16)
            sp.dma_start(beta_r[:], beta.partition_broadcast(P)).then_inc(affine_loaded, 16)
            sp.wait_ge(bo_split, 2)
            sp.dma_start(f32(bo_two[0:1]), f32(bo_hi[:])).then_inc(bo_ready, 16)
            sp.dma_start(f32(bo_two[1:2]), f32(bo_lo[:])).then_inc(bo_ready, 16)
            for i in range(2):
                sp.wait_ge(w_lo, 4 * (i + 1))
                load_x(i, i)

            def body(it, last):
                for r in range(2):
                    c = 2 * it + r
                    if not (last and r == 1):
                        wait(sp, o_lo, Q * (c + 1))
                        load_o(c + 1)
                    for t in range(TT):
                        k = TT * c + t
                        wait(sp, done, k + 1)
                        sp.dma_start(out_v[bass.ds(c, 1), t].rearrange("o p c -> (o p) c"), z[:, t % 2]).then_inc(stored[t % 2], 16)
                    if not last:
                        wait(sp, summed, TT * (c + 1))
                        load_x(c + 2, r)
            with sp.Fori(0, NCH // 2 - 1) as it:
                body(it, False)
            body(NCH // 2 - 1, True)
            for r in range(2):
                sp.wait_ge(stored[r], 16 * NCH * TT // 2)

        @block.tensor
        def _(pe):
            pe.wait_ge(bo_ready, 32)
            pe.wait_ge(ones_set, 2)
            pe.wait_ge(w_lo, CT)

            def body(it):
                for r in range(2):
                    c = 2 * it + r
                    for t in range(TT):
                        k = TT * c + t
                        if t == 0:
                            wait(pe, o_lo, Q * (c + 1))
                        wait(pe, summed, k - 1)
                        tok = slice(t * P, (t + 1) * P)
                        for n in range(NC):
                            cols = slice(n * CH, (n + 1) * CH)
                            bank = acc[t % 2][:, cols]
                            for g in range(CT):
                                for a, w in ((oT_hi[r], wo_hi), (oT_hi[r], wo_lo), (oT_lo[r], wo_hi)):
                                    nc.tensor.matmul(bank, a[:, g, tok], w[:, g, cols],
                                                     start=g == 0 and a is oT_hi[r] and w is wo_hi, stop=False)
                            last = nc.tensor.matmul(bank, ones[:], bo_two[:, cols], start=False, stop=True)
                        last.then_inc(projected, 1)
            body(0)
            with pe.Fori(1, NCH // 2) as it:
                body(it)

        @block.scalar
        def _(act):
            for k in range(CT):
                act.wait_ge(w_loaded[k // 4], 16)
                nc.scalar.activation(wo_hi[:, k], x_res[k // 4][:, k % 4], ACT.Copy).then_inc(w_hi, 1)
            act.wait_ge(bo_loaded, 16)
            nc.scalar.activation(bo_hi[:], bo_row[:], ACT.Copy).then_inc(bo_split, 1)
            act.wait_ge(ones_set, 1)
            nc.scalar.activation(ones[:], ones_f[:], ACT.Copy).then_inc(ones_set, 1)
            act.wait_ge(consts_set, 1)

            def split_hi(c, r, j):
                nc.scalar.activation(oT_hi[r][:, QK * j:QK * (j + 1)].rearrange("p g l -> p (g l)"),
                                     o_in[:, QK * j:QK * (j + 1)].rearrange("p g l -> p (g l)"), ACT.Copy).then_inc(o_hi, 1)

            act.wait_ge(o_loaded, 16)
            for j in range(Q):
                split_hi(0, 0, j)

            def body(it, last):
                for r in range(2):
                    c = 2 * it + r
                    for t in range(TT):
                        k = TT * c + t
                        wait(act, measured, k + 1)
                        nc.scalar.activation(std[:, t % 2:t % 2 + 1], mv[:, t % 2, 1:2], ACT.Sqrt, bias=eps[:]).then_inc(rooted, 1)
                        wait(act, centred, k + 1)
                        wait(act, stored[t % 2], 16 * (TT // 2 * c + t // 2))
                        nc.scalar.activation(z[:, t % 2], y[:, t % 2], ACT.Identity, scale=rstd[:, t % 2:t % 2 + 1],
                                             bias=shift[:, t % 2:t % 2 + 1]).then_inc(scaled, 1)
                        if not (last and r == 1):
                            if t == 0:
                                wait(act, o_loaded, 16 * (c + 2))
                                wait(act, projected, TT * c)
                            split_hi(c + 1, 1 - r, t)
            body(0, False)
            with act.Fori(1, NCH // 2 - 1) as it:
                body(it, False)
            body(NCH // 2 - 1, True)

        @block.vector
        def _(dve):
            nc.vector.memset(ones_f[:], 1.0).then_inc(ones_set, 1)
            nc.vector.memset(eps[:], EPS).then_inc(consts_set, 1)
            for k in range(CT):
                dve.wait_ge(w_hi, k + 1)
                nc.vector.tensor_tensor(wo_lo[:, k], x_res[k // 4][:, k % 4], f32(wo_hi[:, k]), ALU.subtract).then_inc(w_lo, 1)
            dve.wait_ge(bo_split, 1)
            nc.vector.tensor_tensor(bo_lo[:], bo_row[:], f32(bo_hi[:]), ALU.subtract).then_inc(bo_split, 1)

            def split_lo(c, r, j):
                flat = lambda a: a[:, QK * j:QK * (j + 1)].rearrange("p g l -> p (g l)")
                wait(dve, o_hi, Q * c + j + 1)
                nc.vector.tensor_tensor(flat(oT_lo[r]), flat(o_in), f32(flat(oT_hi[r])), ALU.subtract).then_inc(o_lo, 1)

            for j in range(Q):
                split_lo(0, 0, j)
            dve.wait_ge(affine_loaded, 32)

            def body(it, last):
                for r in range(2):
                    c = 2 * it + r
                    for t in range(TT):
                        k, s = TT * c + t, t % 2
                        if t == 0:
                            wait(dve, x_loaded[r], 16 * (it + 1))
                        wait(dve, projected, k + 1)
                        nc.vector.tensor_tensor(y[:, s], acc[s][:], x_res[r][:, t], ALU.add).then_inc(summed, 1)
                        wait(dve, summed, k + 1)
                        for n in range(NC):
                            nc.vector.bn_stats(stats[:, n], y[:, s, n * CH:(n + 1) * CH]).then_inc(statted, 1)
                        wait_before(dve, statted, NC * (k + 1), seen)
                        nc.vector.bn_aggr(mv[:, s], stats[:].rearrange("p n s -> p (n s)")).then_inc(measured, 1)
                        wait(dve, rooted, k + 1)
                        nc.vector.reciprocal(rstd[:, s:s + 1], std[:, s:s + 1]).then_inc(inverted, 1)
                        wait(dve, inverted, k + 1)
                        nc.vector.tensor_scalar(shift[:, s:s + 1], mv[:, s, 0:1], rstd[:, s:s + 1], -1.0, ALU.mult, ALU.mult).then_inc(centred, 1)
                        wait(dve, scaled, k + 1)
                        nc.vector.tensor_tensor(z[:, s], z[:, s], gamma_r[:], ALU.mult).then_inc(weighed, 1)
                        wait(dve, weighed, k + 1)
                        nc.vector.tensor_tensor(z[:, s], z[:, s], beta_r[:], ALU.add).then_inc(done, 1)
                        if not (last and r == 1):
                            split_lo(c + 1, 1 - r, t)
            with dve.Fori(0, NCH // 2 - 1) as it:
                body(it, False)
            body(NCH // 2 - 1, True)



_INS = ["x", "ctx_2048", "mask_Bx1xSxS2_ff0", "L0_xattn_Wq", "L0_xattn_bq", "L0_xattn_Wk", "L0_xattn_bk", "L0_xattn_Wv",
        "L0_xattn_bv", "L0_xattn_Wo", "L0_xattn_bo", "L0_xattn_gamma", "L0_xattn_beta"]


def cross_attention(nc, x, context, mask, wq, bq, wk, bk, wv, bv, wo, bo, gamma, beta, ident, out):
    dram = lambda name, shape: nc.dram_tensor(name, shape, F32, kind="Internal").ap()
    scratch = {"q_hi": dram("q_hi_s", [NCH, KVH, P, CH]), "q_lo": dram("q_lo_s", [NCH, KVH, P, CH]),
               "k_hi": dram("k_hi_s", [NCH, E, CH]), "k_lo": dram("k_lo_s", [NCH, E, CH]),
               "v": dram("v_s", [B * L, E]), "o": dram("o_s", [NCH, KVH, P, CH])}
    with nc.sbuf_tensor("flags", [P, PAIRS], I32) as flags:
        project_qkv(nc, x, context, mask, wq, bq, wk, bk, wv, bv, ident, scratch, flags)
        attend(nc, mask, ident, scratch, flags)
    project_out(nc, x, wo, bo, gamma, beta, scratch, out)


def kernel(**inputs):
    import numpy as _np
    import concourse.bacc as _bacc
    from concourse.bass_utils import run_bass_kernel_spmd as _run

    nc = _bacc.Bacc("TRN2", target_bir_lowering=False, num_devices=1, dynamic_dma_scratch_size=1024)
    arrays = {f"in_{name}": _np.ascontiguousarray(inputs[name]) for name in _INS}
    arrays["in_identity"] = _np.eye(P, dtype=_np.float32)
    args = [nc.dram_tensor(name, a.shape, mybir.dt.from_np(a.dtype), kind="ExternalInput").ap() for name, a in arrays.items()]
    out = nc.dram_tensor("out_0", (B, L, H), F32, kind="ExternalOutput").ap()
    cross_attention(nc, *args, out)
    result = _run(nc, [arrays], core_ids=[0])
    return result.results[0]["out_0"]
```

```python
from contextlib import ExitStack

import concourse.bass as bass
from concourse import mybir

F32 = mybir.dt.float32
F32R = mybir.dt.float32r
BF16 = mybir.dt.bfloat16
I32 = mybir.dt.int32
ALU = mybir.AluOpType
ACT = mybir.ActivationFunctionType
AX = mybir.AxisListType

P = 128
B, L, H = 4, 1024, 1024
KVH, HEADS = 8, 4
D = H // (KVH * HEADS)
E = KVH * D
SCALE = float(D) ** -0.5
EPS = 1e-6
CH = 512
NCH = B * L // CH
HALVES = L // CH
CT = H // P
TT = CH // P
NG = B * KVH
ST = L // P
PAIRS = NG // 2
LOWEST = -3.4028234663852886e38


def wait(engine, semaphore, value):
    if not isinstance(value, int) or value > 0:
        engine.wait_ge(semaphore, value)


def wait_before(engine, semaphore, value, counter):
    wait(engine, semaphore, value)
    engine.sem_inc(counter, 1)


def f32(ap):
    return ap.bitcast(F32)



def project_qkv(nc, x, ctx_in, mask, wq, bq, wk, bk, wv, bv, ident_dram, scratch, flags):
    x_v = x.rearrange("b (n t p) c -> (b n) p t c", t=TT, p=P)
    c_v = ctx_in.rearrange("b (n t p) c -> (b n) p t c", t=TT, p=P)
    m_v = mask.rearrange("b o (n t p) s -> (b o n) p t s", t=TT, p=P)
    wq_v = wq.rearrange("(k p) n -> p k n", p=P)
    wk_v = wk.rearrange("(k p) n -> p k n", p=P)
    wv_v = wv.rearrange("(k p) n -> p k n", p=P)
    v_v = scratch["v"].rearrange("(i t p) e -> i t p e", t=TT, p=P)
    q_hi_v, q_lo_v = scratch["q_hi"], scratch["q_lo"]
    k_hi_v, k_lo_v = scratch["k_hi"], scratch["k_lo"]

    with ExitStack() as st:
        sb = lambda name, shape, dt: st.enter_context(nc.sbuf_tensor(name, shape, dt))
        sem = lambda name: st.enter_context(nc.semaphore(name))
        x_tok = sb("x_tok", [P, TT, H], F32)
        c_tok = sb("c_tok", [P, TT, H], F32)
        m_tok = sb("m_tok", [P, TT, H], F32)
        xT_hi, xT_lo = sb("xT_hi", [P, CT, CH], F32R), sb("xT_lo", [P, CT, CH], F32R)
        cT_hi, cT_lo = sb("cT_hi", [P, CT, CH], F32R), sb("cT_lo", [P, CT, CH], F32R)
        wq_hi, wq_lo = sb("wq_hi", [P, CT, H], F32R), sb("wq_lo", [P, CT, H], F32R)
        wk_hi, wk_lo = sb("wk_hi", [P, CT, E], F32R), sb("wk_lo", [P, CT, E], F32R)
        wv_hi, wv_lo = sb("wv_hi", [P, CT, E], F32R), sb("wv_lo", [P, CT, E], F32R)
        out_hi, out_lo = sb("qk_out_hi", [P, 2, CH], F32R), sb("qk_out_lo", [P, 2, CH], F32R)
        v_out = sb("v_out", [P, 2, E], F32)
        ident = sb("ident1", [P, P], F32)
        ones = sb("ones1", [P, P], F32)
        bq_c = sb("bq_c", [P, CT], F32)
        bk_c = sb("bk_c", [P, 2], F32)
        bks_c = sb("bks_c", [P, 2], F32)
        bv_r = sb("bv_r", [P, E], F32)
        absum = sb("absum", [P, NCH * TT], F32)
        bsum = sb("bsum", [P, B], F32)
        tr = [st.enter_context(nc.psum_tensor(f"tr{i}", [P, CH], F32)) for i in range(2)]
        pq = [st.enter_context(nc.psum_tensor(f"pq{i}", [P, CH], F32)) for i in range(4)]
        pkv = [st.enter_context(nc.psum_tensor(f"pkv{i}", [P, CH], F32)) for i in range(2)]

        x_loaded, c_loaded, m_loaded = sem("x_loaded"), sem("c_loaded"), sem("m_loaded")
        w_loaded = [sem(f"w_loaded{i}") for i in range(4)]
        x_first, ident_loaded, consts_loaded = sem("x_first"), sem("ident_loaded"), sem("consts_loaded")
        w_hi, w_lo = sem("w_hi"), sem("w_lo")
        tr_ready, tr_hi, tr_lo = sem("tr_ready"), sem("tr_hi"), sem("tr_lo")
        out_ready, hi_done, out_done = sem("out_ready"), sem("hi_done"), sem("out_done")
        qk_stored = [sem(f"qk_stored{i}") for i in range(2)]
        v_stored = [sem(f"v_stored{i}") for i in range(2)]
        mask_summed, small_done, flag_ready = sem("mask_summed"), sem("small_done"), sem("flag_ready")
        ones_set = sem("ones_set")

        T, OUT, QK, V = 2 * CT, 14, 10, 4
        tr_ctx = lambda i, k: CT + T * i + k
        tr_x = lambda i, k: T * i + k

        w_tok = [tok[:].rearrange("p t (h c) -> p (t h) c", c=CH) for tok in (m_tok, c_tok)]
        wkv = x_tok[:].rearrange("p t c -> p (t c)").rearrange("p (w k e) -> p w k e", w=2, e=E)
        W = 2 * CT

        def steps(first, last):
            for m in range(CT):
                for k in ((2 * m - CT, 2 * m - CT + 1) if first else (m,)):
                    if k >= 0:
                        yield "tc", k
                yield "q", m
            x_at = [(0, 1), (2, 3), (4, 5), (6,), (7,), ()]
            for n in range(6):
                yield ("k", n) if n < 2 else ("v", n - 2)
                if not last:
                    for k in x_at[n]:
                        yield "tx", k

        def iterations(engine, body):
            body(0, True, False)
            with engine.Fori(1, NCH - 1) as i:
                body(i, False, False)
            body(NCH - 1, False, True)

        block = st.enter_context(nc.Block())

        @block.sync
        def _(sp):
            half, low = H // 2, CT // 2
            sp.dma_start(ident[:], ident_dram).then_inc(ident_loaded, 16)
            sp.dma_start(x_tok[:, :, 0:half], x_v[0, :, :, 0:half]).then_inc(x_first, 16)
            sp.dma_start(x_tok[:, :, half:H], x_v[0, :, :, half:H]).then_inc(x_loaded, 16)
            sp.dma_start(w_tok[0][:, 0:low], wq_v[:, 0:low, 0:CH]).then_inc(w_loaded[0], 16)
            sp.dma_start(w_tok[0][:, low:CT], wq_v[:, low:CT, 0:CH]).then_inc(w_loaded[1], 16)
            sp.dma_start(w_tok[1], wq_v[:, :, CH:H]).then_inc(w_loaded[2], 16)
            sp.dma_start(bq_c[:], bq.rearrange("(m p) -> p m", p=P), allow_slow_non_contiguous=True).then_inc(consts_loaded, 16)
            sp.dma_start(bk_c[:], bk.rearrange("(m p) -> p m", p=P), allow_slow_non_contiguous=True).then_inc(consts_loaded, 16)
            sp.dma_start(bv_r[:], bv.partition_broadcast(P)).then_inc(consts_loaded, 16)
            sp.wait_ge(tr_ready, CT)
            sp.dma_start(wkv[:, 0], wk_v).then_inc(w_loaded[3], 16)
            sp.dma_start(wkv[:, 1], wv_v).then_inc(w_loaded[3], 16)
            sp.wait_ge(w_lo, CT)
            sp.dma_start(m_tok[:], m_v[0]).then_inc(m_loaded, 16)
            sp.wait_ge(w_lo, W)
            sp.dma_start(c_tok[:], c_v[0]).then_inc(c_loaded, 16)

            def body(i, first, last):
                def load_x():
                    src = x_v[bass.ds(i + 1, 1)].rearrange("o p t c -> (o p) t c")
                    sp.dma_start(x_tok[:], src).then_inc(x_loaded, 16)

                if not first and not last:
                    wait(sp, tr_ready, tr_x(i, CT))
                    load_x()
                for what, n in steps(first, last):
                    if what in "qk":
                        j = n if what == "q" else CT + n
                        wait(sp, out_done, OUT * i + j + 1)
                        hi, lo = (q_hi_v, q_lo_v) if what == "q" else (k_hi_v, k_lo_v)
                        for part, dram in ((out_hi, hi), (out_lo, lo)):
                            to = dram[bass.ds(i, 1), n] if what == "q" else dram[bass.ds(i, 1), n * P:(n + 1) * P]
                            sp.dma_start(to.rearrange("o p l -> (o p) l"), f32(part[:, j % 2])).then_inc(qk_stored[j % 2], 16)
                    if first and what == "q" and n == TT:
                        wait(sp, w_lo, W + 2)
                        load_x()
                    if what == "v":
                        wait(sp, out_done, OUT * i + QK + n + 1)
                        sp.dma_start(v_v[bass.ds(i, 1), n].rearrange("o p e -> (o p) e"), v_out[:, n % 2]).then_inc(v_stored[n % 2], 16)
                    if what == ("tc" if first else "q") and n == CT - 1 and not last:
                        wait(sp, tr_ready, tr_ctx(i, CT))
                        sp.dma_start(c_tok[:], c_v[bass.ds(i + 1, 1)].rearrange("o p t c -> (o p) t c")).then_inc(c_loaded, 16)
                    if what == "k" and n == 0 and not last:
                        wait(sp, mask_summed, TT * (i + 1))
                        sp.dma_start(m_tok[:], m_v[bass.ds(i + 1, 1)].rearrange("o p t c -> (o p) t c")).then_inc(m_loaded, 16)
            iterations(sp, body)
            for r in range(2):
                sp.wait_ge(qk_stored[r], NCH * QK // 2 * 32)
                sp.wait_ge(v_stored[r], NCH * V // 2 * 16)

        @block.tensor
        def _(pe):
            def transpose_tile(tok, at, k):
                wait(pe, tr_lo, at - 1)
                for t in range(TT):
                    last = nc.tensor.transpose(tr[k % 2][:, t * P:(t + 1) * P], tok[:, t, k * P:(k + 1) * P], ident[:])
                last.then_inc(tr_ready, 1)

            def product(bank, terms, splitting=False):
                for n, (a, b) in enumerate(terms):
                    if splitting and n % 3 == 0:
                        pe.wait_ge(w_lo, n // 3 + 1)
                    last = nc.tensor.matmul(bank, a, b, start=n == 0, stop=n == len(terms) - 1)
                last.then_inc(out_ready, 1)

            pe.wait_ge(ident_loaded, 16)
            for k in range(CT):
                pe.wait_ge(x_first if k < CT // 2 else x_loaded, 16)
                transpose_tile(x_tok, k, k)

            def body(i, first, last):
                for what, n in steps(first, last):
                    if what == "tc":
                        if n == 0:
                            wait(pe, c_loaded, 16 * (i + 1))
                        transpose_tile(c_tok, tr_ctx(i, n), n)
                    if what == "tx":
                        if n == 0:
                            wait(pe, x_loaded, 16 * (i + 2))
                        transpose_tile(x_tok, tr_x(i + 1, n), n)
                    if what == "q":
                        if n == 0:
                            wait(pe, tr_lo, tr_x(i, CT))
                        if first and n == TT:
                            wait(pe, w_lo, W)
                        wait(pe, out_done, OUT * i + n - 3 if n >= 4 else OUT * (i - 1) + n + 5)
                        cols = slice(n * P, (n + 1) * P)
                        product(pq[n % 4][:], [(w[:, k, cols], t[:, k]) for k in range(CT)
                                               for w, t in ((wq_hi, xT_hi), (wq_lo, xT_hi), (wq_hi, xT_lo))],
                                splitting=first and n == 0)
                    if what == "k":
                        if n == 0:
                            wait(pe, tr_lo, tr_ctx(i, CT))
                            if first:
                                wait(pe, w_lo, W + 2)
                        wait(pe, out_done, OUT * i + n - 1)
                        cols = slice(n * P, (n + 1) * P)
                        product(pkv[n % 2][:], [(w[:, k, cols], t[:, k]) for k in range(CT)
                                                for w, t in ((wk_hi, cT_hi), (wk_lo, cT_hi), (wk_hi, cT_lo))])
                    if what == "v":
                        wait(pe, out_done, OUT * i + CT + n + 1)
                        cols = slice(n * P, (n + 1) * P)
                        product(pkv[n % 2][:, 0:E], [(t[:, k, cols], w[:, k]) for k in range(CT)
                                                     for w, t in ((wv_hi, cT_hi), (wv_lo, cT_hi), (wv_hi, cT_lo))])
            iterations(pe, body)
            pe.wait_ge(ones_set, 1)
            pe.wait_ge(mask_summed, NCH * TT)
            nc.tensor.matmul(tr[0][:, 0:NCH * TT], ones[:], absum[:], start=True, stop=True).then_inc(flag_ready, 1)

        @block.scalar
        def _(act):
            def transposed(at, k, hi):
                wait(act, tr_ready, at + 1)
                nc.scalar.activation(hi[:, k], tr[k % 2][:], ACT.Copy).then_inc(tr_hi, 1)

            def split_wq(half, k):
                act.wait_ge(w_loaded[2 if half else k // (CT // 2)], 16)
                nc.scalar.activation(wq_hi[:, k, half * CH:(half + 1) * CH], w_tok[half][:, k], ACT.Copy).then_inc(w_hi, 1)

            low = CT // 2
            for k in range(low):
                transposed(k, k, xT_hi)
            for k in range(low):
                transposed(low + k, low + k, xT_hi)
                split_wq(0, k)
            for k in range(low, 2 * CT):
                split_wq(k // CT, k % CT)
            act.wait_ge(consts_loaded, 48)

            def split_wkv():
                act.wait_ge(w_loaded[3], 32)
                nc.scalar.activation(wk_hi[:], wkv[:, 0], ACT.Copy, scale=SCALE).then_inc(w_hi, 1)
                nc.scalar.activation(wv_hi[:], wkv[:, 1], ACT.Copy).then_inc(w_hi, 1)
                act.wait_ge(small_done, 1)

            def body(i, first, last):
                for what, n in steps(first, last):
                    if what == "tc":
                        if n == 0:
                            wait(act, out_ready, OUT * i)
                        transposed(tr_ctx(i, n), n, cT_hi)
                    if what == "tx":
                        if n == 0:
                            wait(act, out_ready, OUT * i + CT)
                        transposed(tr_x(i + 1, n), n, xT_hi)
                    if what in "qk":
                        j = n if what == "q" else CT + n
                        bank, bias = (pq[n % 4], bq_c) if what == "q" else (pkv[n % 2], bks_c)
                        wait(act, out_ready, OUT * i + j + 1)
                        wait(act, qk_stored[j % 2], 32 * (QK // 2 * i + j // 2))
                        nc.scalar.activation(out_hi[:, j % 2], bank[:], ACT.Identity, bias=bias[:, n:n + 1]).then_inc(hi_done, 1)
                        if first and what == "q" and n == TT:
                            split_wkv()
            iterations(act, body)

        @block.vector
        def _(dve):
            def transposed(at, k, hi, lo):
                wait(dve, tr_hi, at + 1)
                nc.vector.tensor_tensor(lo[:, k], tr[k % 2][:], f32(hi[:, k]), ALU.subtract).then_inc(tr_lo, 1)

            def split_wq(half, k):
                cols = slice(half * CH, (half + 1) * CH)
                dve.wait_ge(w_hi, CT * half + k + 1)
                nc.vector.tensor_tensor(wq_lo[:, k, cols], w_tok[half][:, k], f32(wq_hi[:, k, cols]), ALU.subtract).then_inc(w_lo, 1)

            nc.vector.memset(ones[:], 1.0).then_inc(ones_set, 1)
            low = CT // 2
            for k in range(low):
                transposed(k, k, xT_hi, xT_lo)
            for k in range(low):
                transposed(low + k, low + k, xT_hi, xT_lo)
                split_wq(0, k)
            for k in range(low, 2 * CT):
                split_wq(k // CT, k % CT)
            dve.wait_ge(consts_loaded, 48)
            nc.vector.tensor_scalar(bks_c[:], bk_c[:], SCALE, None, ALU.mult).then_inc(small_done, 1)
            dve.wait_ge(small_done, 1)

            def split_wkv():
                dve.wait_ge(w_hi, W + 1)
                nc.vector.scalar_tensor_tensor(wk_lo[:], wkv[:, 0], SCALE, f32(wk_hi[:]), ALU.mult, ALU.subtract).then_inc(w_lo, 1)
                dve.wait_ge(w_hi, W + 2)
                nc.vector.tensor_tensor(wv_lo[:], wkv[:, 1], f32(wv_hi[:]), ALU.subtract).then_inc(w_lo, 1)

            def body(i, first, last):
                for what, n in steps(first, last):
                    if what == "tc":
                        transposed(tr_ctx(i, n), n, cT_hi, cT_lo)
                    if what == "tx":
                        transposed(tr_x(i + 1, n), n, xT_hi, xT_lo)
                    if what in "qk":
                        j = n if what == "q" else CT + n
                        bank, bias = (pq[n % 4], bq_c) if what == "q" else (pkv[n % 2], bks_c)
                        wait(dve, hi_done, QK * i + j + 1)
                        nc.vector.scalar_tensor_tensor(out_lo[:, j % 2], bank[:], bias[:, n:n + 1], f32(out_hi[:, j % 2]),
                                                       ALU.add, ALU.subtract).then_inc(out_done, 1)
                        if first and what == "q" and n == TT:
                            split_wkv()
                    if what == "v":
                        wait(dve, out_ready, OUT * i + QK + n + 1)
                        wait(dve, v_stored[n % 2], 16 * (V // 2 * i + n // 2))
                        nc.vector.tensor_tensor(v_out[:, n % 2], pkv[n % 2][:, 0:E], bv_r[:], ALU.add).then_inc(out_done, 1)
                    if what == "q" and n >= TT:
                        t = n - TT
                        wait(dve, m_loaded, 16 * (i + 1))
                        nc.vector.tensor_reduce(absum[:, bass.ds(TT * i + t, 1)], m_tok[:, t], AX.X, ALU.add,
                                                apply_absolute_value=True).then_inc(mask_summed, 1)
            iterations(dve, body)
            dve.wait_ge(flag_ready, 1)
            parts = tr[0][:, 0:NCH * TT].rearrange("p (b h) -> p b h", h=HALVES * TT)
            nc.vector.tensor_reduce(bsum[:], parts, AX.X, ALU.add).then_inc(small_done, 1)
            dve.wait_ge(small_done, 2)
            per_batch = PAIRS // B
            nc.vector.tensor_scalar(flags[:].rearrange("p (b r) -> p b r", r=per_batch),
                                    bsum[:].unsqueeze(2).to_broadcast([P, B, per_batch]),
                                    0.0, None, ALU.not_equal).then_inc(small_done, 1)
            dve.wait_ge(small_done, 3)



def attend(nc, mask, ident_dram, scratch, flags):
    q_hi_v = scratch["q_hi"].rearrange("i g (h d) l -> i g d h l", d=D)
    q_lo_v = scratch["q_lo"].rearrange("i g (h d) l -> i g d h l", d=D)
    k_v = {part: scratch[part].rearrange("(b f) e s -> b e f s", f=HALVES) for part in ("k_hi", "k_lo")}
    v_v = scratch["v"].rearrange("(b t p) e -> b p t e", t=ST, p=P)
    o_v = scratch["o"]
    mask_v = mask.rearrange("b o (t p) s -> t (b o) p s", p=P)
    R3 = 3 * D
    R = R3 + 2
    NX = NG * HALVES
    QT = ST // HALVES
    ROWS = QT * HEADS
    ADDS = 5

    PAIR_AT, SUMS_AT, NORM_AT, TURN_AT = 0, 2, 4, 5
    ROWS_AT = (2, 2, 2, 3, 1, 2, 2, 2)
    LEAD = sum(ROWS_AT[NORM_AT:])

    with ExitStack() as st:
        sb = lambda name, shape, dt: st.enter_context(nc.sbuf_tensor(name, shape, dt))
        ps = lambda name, shape: st.enter_context(nc.psum_tensor(name, shape, F32))
        sem = lambda name: st.enter_context(nc.semaphore(name))
        q_st = [sb(f"q_st{i}", [P, HEADS, CH], F32R) for i in range(4)]
        k_max = [sb(f"k_max{u}", [P, L], F32R) for u in range(2)]
        k_exp = [sb(f"k_exp{u}", [P, L], F32R) for u in range(2)]
        v_sb = [sb(f"v_sb{u}", [P, ST, D], F32) for u in range(2)]
        mask_q = sb("mask_q", [P, ST, L], F32)
        mask_k = sb("mask_k", [P, ST, L], F32)
        probs = sb("probs", [P, ST, HEADS, CH], F32)
        key_sum = [sb(f"key_sum{f}", [P, HEADS * CH], F32) for f in range(HALVES)]
        pair_sum = sb("pair_sum", [P, HEADS * CH], F32)
        sums_t, recip_row = sb("sums_t", [P, CH], F32), sb("recip_row", [P, CH // D], F32)
        recip, o_raw, o_n = sb("recip", [P, CH], F32), sb("o_raw", [P, CH], F32), sb("o_n", [P, CH], F32)
        junk = sb("junk", [P, 2, L], BF16)
        row_max = sb("row_max", [P, HALVES, ROWS], F32)
        neg_max = sb("neg_max", [P, P // ROWS, ROWS], F32R)
        neg_max_t = sb("neg_max_t", [2 * ROWS, P], F32)
        ones = sb("ones2", [P, D], F32)
        ident = sb("ident2", [P, P], F32)
        sc_q = [ps(f"sc_q{i}", [P, L]) for i in range(2)]
        sc_k = [ps(f"sc_k{i}", [P, CH]) for i in range(2)]
        out_ps = ps("out_ps", [P, CH])
        misc = ps("misc", [P, CH])

        consts_loaded, consts_set = sem("consts2_loaded"), sem("consts2_set")
        mask_loaded = [sem(f"mask_loaded{t}") for t in range(ST)]
        q_loaded = [sem(f"q_loaded{i}") for i in range(4)]
        km_loaded = [sem(f"km_loaded{u}") for u in range(2)]
        kv_loaded = [sem(f"kv_loaded{u}") for u in range(2)]
        nm_loaded = [sem(f"nm_loaded{i}") for i in range(4)]
        q_scored, q_maxed, seen = sem("q_scored"), sem("q_maxed"), sem("seen2")
        k_scored, k_masked, exp_done = sem("k_scored"), sem("k_masked"), sem("exp_done")
        pv_done, key_added, pair_added = sem("pv_done"), sem("key_added"), sem("pair_added")
        sums_done, raw_out, sums_read, out_ready = sem("sums_done"), sem("raw_out"), sem("sums_read"), sem("o_ready")
        max_split, max_turned, max_ready, o_stored = sem("max_split"), sem("max_turned"), sem("max_ready"), sem("o_stored")
        mk_turned, mk_ready = sem("mk_turned"), sem("mk_ready")
        chain, norm = sem("max_chain"), sem("norm_chain")

        EXPS = HEADS * ST

        def place(it, j):
            return 4 * it + j, j % 4, it + j // 4

        def ahead(it, j, s):
            at = [LEAD + sum(ROWS_AT[:s]) + r for r in range(ROWS_AT[s])]
            rows = [(1 + a // ROWS, a % ROWS) for a in at]
            return [(d, r) for d, r in rows if not isinstance(it, int) or 4 * it + j + d < NX]

        def follows(it, j):
            return not isinstance(it, int) or 4 * it + j + 1 < NX

        def fours(engine, body):
            body(0)
            with engine.Fori(1, NX // 4 - 1) as it:
                body(it)
            body(NX // 4 - 1)

        block = st.enter_context(nc.Block())

        @block.sync
        def _(sp):
            def load_mask(t, b):
                sp.dma_start(mask_q[:, t], mask_v[t, bass.ds(b, 1)].rearrange("o p s -> (o p) s")).then_inc(mask_loaded[t], 16)

            def load_q(it, j):
                x, i, _ = place(it, j)
                b, g = x // (HALVES * KVH), x // HALVES % KVH
                for row, part in ((0, q_hi_v), (1, q_hi_v), (2, q_lo_v)):
                    src = part[bass.ds(b * HALVES + j % HALVES, 1), bass.ds(g, 1)].rearrange("o r d h l -> (o r d) h l")
                    sp.dma_start(f32(q_st[i][row * D:(row + 1) * D]), src).then_inc(q_loaded[i], 16)

            def load_k(n, dst, semaphore):
                b, g = n // KVH, n % KVH
                for row, part in ((0, "k_hi"), (1, "k_lo"), (2, "k_hi")):
                    src = k_v[part][bass.ds(b, 1), bass.ds(g * D, D)].rearrange("o d f s -> (o d) f s")
                    sp.dma_start(f32(dst[row * D:(row + 1) * D]).rearrange("d (f s) -> d f s", f=HALVES), src).then_inc(semaphore, 16)

            def load_v(n, u):
                b, g = n // KVH, n % KVH
                src = v_v[bass.ds(b, 1), :, :, bass.ds(g * D, D)].rearrange("o p t e -> (o p) t e")
                sp.dma_start(v_sb[u][:], src).then_inc(kv_loaded[u], 16)

            def store_o(it, j):
                x, _, _ = place(it, j)
                wait(sp, out_ready, x + 1)
                b, g = x // (HALVES * KVH), x // HALVES % KVH
                dst = o_v[bass.ds(b * HALVES + j % HALVES, 1), bass.ds(g, 1)].rearrange("o r p l -> (o r p) l")
                sp.dma_start(dst, o_n[:]).then_inc(o_stored, 16)

            def store_max(it, j):
                x, i, _ = place(it, j)
                wait(sp, max_ready, x + 1)
                for part in range(2):
                    sp.dma_start(f32(q_st[i][R3 + part:R3 + part + 1]).rearrange("o h (t l) -> o (h t) l", l=P),
                                 neg_max_t[part * ROWS:(part + 1) * ROWS]).then_inc(nm_loaded[i], 16)

            load_q(0, 0)
            load_k(0, k_max[0], km_loaded[0])
            load_mask(0, 0)
            sp.dma_start(ident[:], ident_dram).then_inc(consts_loaded, 16)
            for t in range(1, QT):
                load_mask(t, 0)
            load_q(0, 1)
            load_k(0, k_exp[0], kv_loaded[0])
            load_v(0, 0)
            for t in range(QT, ST):
                load_mask(t, 0)
            load_q(0, 2)
            load_k(1, k_max[1], km_loaded[1])
            store_max(0, 0)

            def body(it):
                first, last = isinstance(it, int) and it == 0, isinstance(it, int) and it > 0
                for j in range(4):
                    x, _, _ = place(it, j)
                    u, f = divmod(j, 2)
                    n = 2 * it + u
                    if not (last and j > 0):
                        wait(sp, k_scored, EXPS * x)
                        load_q(it, j + 3)
                    if f == 0 and not (last and u == 1):
                        load_k(n + 1, k_exp[1 - u], kv_loaded[1 - u])
                        wait(sp, pv_done, ST * x)
                        load_v(n + 1, 1 - u)
                    if not (last and j == 3):
                        store_max(it, j + 1)
                    if not (first and j == 0):
                        store_o(it, j - 1)
                    if f == 0 and not last:
                        wait(sp, q_maxed, ROWS * (x + 2))
                        load_k(n + 2, k_max[u], km_loaded[u])
                    if j in (1, 2) and not first and not last:
                        with sp.If((it % (PAIRS // B)) == PAIRS // B - 1):
                            wait(sp, q_maxed, ROWS * (x + 2))
                            for t in range(QT):
                                load_mask(QT * (j - 1) + t, (it + 1) // (PAIRS // B))
            fours(sp, body)
            store_o(NX // 4 - 1, 3)
            sp.wait_ge(o_stored, 16 * NX)

        @block.gpsimd
        def _(pool):
            def body(it):
                for j in range(4):
                    x, _, _ = place(it, j)
                    total = key_sum[j % 2][:]
                    flat = lambda t: probs[:, t].rearrange("p h l -> p (h l)")
                    for k in range(ADDS):
                        wait(pool, exp_done, EXPS * x + HEADS * (k + 2))
                        if k == 0:
                            wait(pool, sums_done, x - 1)
                        else:
                            wait(pool, key_added, ADDS * x + k)
                        nc.gpsimd.tensor_tensor(total, flat(0) if k == 0 else total, flat(k + 1), ALU.add).then_inc(key_added, 1)
            fours(pool, body)

        @block.tensor
        def _(pe):
            def score_q(it, j, r):
                x, i, turn = place(it, j)
                t, h = divmod(r, HEADS)
                if r == 0:
                    wait(pe, q_loaded[i], 48 * (turn + 1))
                    if i % 2 == 0:
                        wait(pe, km_loaded[i // 2], 48 * (turn + 1))
                wait(pe, q_maxed, ROWS * x + r - 1)
                for f in range(HALVES):
                    last = nc.tensor.matmul(sc_q[r % 2][:, f * CH:(f + 1) * CH], q_st[i][0:R3, h, t * P:(t + 1) * P],
                                            k_max[i // 2][0:R3, f * CH:(f + 1) * CH], start=True, stop=True)
                last.then_inc(q_scored, 1)

            def turn_max(x):
                wait(pe, max_split, x + 1)
                wait(pe, sums_read, x - 1)
                nc.tensor.transpose(misc[:, 0:P], f32(neg_max[:]).rearrange("p a c -> p (a c)"), ident[:]).then_inc(max_turned, 1)

            def score_k(it, j, s, h):
                x, i, _ = place(it, j)
                wait(pe, exp_done, EXPS * x + HEADS * s + h - 1)
                nc.tensor.matmul(sc_k[h % 2][:], k_exp[i // 2][0:R, s * P:(s + 1) * P], q_st[i][0:R, h],
                                 start=True, stop=True).then_inc(k_scored, 1)

            def times_v(it, j, s):
                x, i, _ = place(it, j)
                wait(pe, exp_done, EXPS * x + HEADS * (s + 1))
                if s == 0:
                    wait(pe, raw_out, x)
                for h in range(HEADS):
                    last = nc.tensor.matmul(out_ps[h * D:(h + 1) * D], v_sb[i // 2][:, s], probs[:, s, h],
                                            start=s == 0, stop=s == ST - 1, tile_position=(0, h * D))
                last.then_inc(pv_done, 1)

            def sum_keys(x, f, part):
                if part == 0:
                    wait(pe, pair_added, 2 * (x + 1))
                    if not (isinstance(x, int) and x == NX - 1):
                        wait(pe, max_ready, x + 2)
                else:
                    wait(pe, key_added, ADDS * (x + 1))
                src = key_sum[f] if part else pair_sum
                for h in range(HEADS):
                    last = nc.tensor.matmul(misc[h * D:(h + 1) * D], ones[:], src[:, h * CH:(h + 1) * CH], start=part == 0,
                                            stop=part == 1, tile_position=(0, h * D))
                if part == 1:
                    last.then_inc(sums_done, 1)

            def turn_mask(it):
                for t in range(ST):
                    wait(pe, mask_loaded[t], 16 * (it // (PAIRS // B) + 1))
                for m in range(2 * ST):
                    t, f = divmod(m, 2)
                    wait(pe, mk_ready, 2 * ST * it + m)
                    for r in range(4):
                        last = nc.tensor.transpose(misc[:, r * P:(r + 1) * P], mask_q[:, 4 * f + r, t * P:(t + 1) * P], ident[:])
                    last.then_inc(mk_turned, 1)

            pe.wait_ge(consts_set, 4)
            for a in range(ROWS + LEAD):
                score_q(0, a // ROWS, a % ROWS)
                if a == ROWS:
                    pe.wait_ge(consts_loaded, 16)
                    turn_max(0)

            def body(it):
                first = isinstance(it, int) and it == 0
                has_mask = pe.value_load(flags[0:1, bass.ds(it, 1)], min_val=0, max_val=1)
                with pe.If(has_mask != 0):
                    wait(pe, sums_read, 4 * it - 1)
                    wait(pe, max_ready, 4 * it + 1)
                    turn_mask(it)
                with pe.Else():
                    wait(pe, mk_turned, 2 * ST * it)
                    pe.sem_inc(mk_turned, 2 * ST)
                for j in range(4):
                    x, i, turn = place(it, j)
                    for s in range(ST):
                        if s == 0:
                            if j % 2 == 0:
                                wait(pe, kv_loaded[i // 2], 64 * (turn + 1))
                            wait(pe, nm_loaded[i], 32 * (turn + 1))
                        rows = ahead(it, j, s)
                        if s == TURN_AT and follows(it, j):
                            turn_max(x + 1)
                        score_k(it, j, s, 0)
                        score_k(it, j, s, 1)
                        if s > 0:
                            times_v(it, j, s - 1)
                        elif not (first and j == 0):
                            times_v(it, j - 1, ST - 1)
                        for d, r in rows[:-2]:
                            score_q(it, j + d, r)
                        score_k(it, j, s, 2)
                        score_k(it, j, s, 3)
                        for d, r in rows[-2:-1]:
                            score_q(it, j + d, r)
                        if SUMS_AT <= s < SUMS_AT + 2 and not (first and j == 0):
                            sum_keys(x - 1, (j - 1) % 2, s - SUMS_AT)
                        for d, r in rows[-1:]:
                            score_q(it, j + d, r)
            fours(pe, body)
            times_v(NX // 4 - 1, 3, ST - 1)
            wait(pe, sums_read, NX - 1)
            for part in range(2):
                sum_keys(NX - 1, 1, part)

        @block.scalar
        def _(act):
            def exponentials(it, j, s, h, masked):
                x, _, _ = place(it, j)
                if h == 0 and not (isinstance(it, int) and it == 0 and j == 0):
                    wait(act, pv_done, ST * (x - 1) + s + 1)
                    if s <= ADDS:
                        wait(act, key_added, ADDS * (x - 1) + max(s, 1))
                    elif s == ADDS + 1:
                        wait(act, pair_added, 2 * x)
                wait(act, k_masked if masked else k_scored, EXPS * x + HEADS * s + h + 1)
                nc.scalar.activation(probs[:, s, h], sc_k[h % 2][:], ACT.Exp).then_inc(exp_done, 1)

            def read_out(x):
                wait(act, pv_done, ST * (x + 1))
                wait(act, out_ready, x)
                nc.scalar.activation(o_raw[:], out_ps[:], ACT.Copy).then_inc(raw_out, 1)

            def read_max(it, j):
                x, _, _ = place(it, j)
                wait(act, max_turned, x + 1)
                if not (isinstance(it, int) and 4 * it + j == 0):
                    wait(act, nm_loaded[(j - 1) % 4], 32 * (it + (j - 1) // 4 + 1))
                nc.scalar.activation(neg_max_t[:], misc[0:2 * ROWS, 0:P], ACT.Copy).then_inc(max_ready, 1)

            read_max(0, 0)

            def halves(it, masked):
                first = isinstance(it, int) and it == 0
                for j in range(4):
                    x, _, _ = place(it, j)
                    for s in range(ST):
                        for h in range(HEADS):
                            exponentials(it, j, s, h, masked)
                            if s == 0 and h == 2 and not (first and j == 0):
                                read_out(x - 1)
                            if s == TURN_AT and h == 0 and follows(it, j):
                                read_max(it, j + 1)

            def body(it):
                has_mask = act.value_load(flags[0:1, bass.ds(it, 1)], min_val=0, max_val=1)
                with act.If(has_mask != 0):
                    wait(act, k_masked, 4 * EXPS * it)
                    for m in range(2 * ST):
                        t, f = divmod(m, 2)
                        wait(act, mk_turned, 2 * ST * it + m + 1)
                        nc.scalar.activation(mask_k[:, t, f * CH:(f + 1) * CH], misc[:], ACT.Copy).then_inc(mk_ready, 1)
                    halves(it, True)
                with act.Else():
                    wait(act, mk_ready, 2 * ST * it)
                    act.sem_inc(mk_ready, 2 * ST)
                    halves(it, False)
            fours(act, body)
            read_out(NX - 1)

        @block.vector
        def _(dve):
            nc.vector.memset(ones[:], 1.0).then_inc(consts_set, 1)
            nc.vector.memset(f32(neg_max[:, 2:]), 0.0).then_inc(consts_set, 1)
            for u in range(2):
                nc.vector.memset(f32(k_exp[u][R3:R]), 1.0).then_inc(consts_set, 1)

            def maximum(it, j, r):
                x, _, turn = place(it, j)
                t, h = divmod(r, HEADS)
                tile = j % 2 * QT + t
                if h == 0:
                    wait(dve, mask_loaded[tile], 16 * (turn // (PAIRS // B) + 1))
                wait_before(dve, q_scored, ROWS * x + r + 1, seen)
                nc.vector.tensor_tensor_reduce(out=junk[:, r % 2], in0=sc_q[r % 2][:], in1=mask_q[:, tile],
                                               scale=1.0, scalar=LOWEST, op0=ALU.add, op1=ALU.max,
                                               accum_out=row_max[:, j % 2, h * QT + t:h * QT + t + 1]).then_inc(q_maxed, 1)

            def split_max(x, f):
                wait(dve, q_maxed, ROWS * (x + 1))
                wait(dve, max_turned, x)
                nc.vector.tensor_scalar(neg_max[:, 0], row_max[:, f], -1.0, None, ALU.mult).then_inc(chain, 1)
                wait(dve, chain, x + 1)
                nc.vector.scalar_tensor_tensor(neg_max[:, 1], row_max[:, f], -1.0, f32(neg_max[:, 0]), ALU.mult,
                                               ALU.subtract).then_inc(max_split, 1)

            def invert(x):
                wait(dve, sums_done, x + 1)
                nc.vector.transpose(sums_t[:], misc[:]).then_inc(sums_read, 1)
                wait(dve, sums_read, x + 1)
                nc.vector.reciprocal(recip_row[:], sums_t[:].rearrange("p (j c) -> p j c", c=D)[:, :, 0]).then_inc(norm, 1)
                wait(dve, norm, 2 * x + 1)
                nc.vector.transpose(recip[:], recip_row[:].unsqueeze(2).to_broadcast([P, CH // D, D])).then_inc(norm, 1)

            def scale_out(x):
                wait(dve, norm, 2 * x + 2)
                wait(dve, raw_out, x + 1)
                wait(dve, o_stored, 16 * x)
                nc.vector.tensor_tensor(o_n[:], o_raw[:], recip[:], ALU.mult).then_inc(out_ready, 1)

            def add_pair(x, half):
                if half == 0:
                    wait(dve, exp_done, EXPS * (x + 1))
                    wait(dve, sums_done, x)
                flat = lambda t: probs[:, t].rearrange("p h l -> p (h l)")[:, half * L:(half + 1) * L]
                nc.vector.tensor_tensor(pair_sum[:, half * L:(half + 1) * L], flat(ADDS + 1), flat(ADDS + 2), ALU.add).then_inc(pair_added, 1)

            def add_mask(x, j, s, h):
                wait(dve, k_scored, EXPS * x + HEADS * s + h + 1)
                m = mask_k[:, s, j % 2 * CH:(j % 2 + 1) * CH]
                nc.vector.tensor_tensor(sc_k[h % 2][:], sc_k[h % 2][:], m, ALU.add).then_inc(k_masked, 1)

            for a in range(ROWS + LEAD):
                maximum(0, a // ROWS, a % ROWS)
                if a == ROWS - 1:
                    split_max(0, 0)

            def halves(it, masked):
                first = isinstance(it, int) and it == 0
                for j in range(4):
                    x, _, _ = place(it, j)
                    for s in range(ST):
                        rows = ahead(it, j, s)
                        if masked:
                            for h in range(HEADS):
                                add_mask(x, j, s, h)
                        if s == NORM_AT and not (first and j == 0):
                            invert(x - 1)
                        if PAIR_AT <= s < PAIR_AT + 2 and not (first and j == 0):
                            add_pair(x - 1, s - PAIR_AT)
                        for d, r in rows:
                            maximum(it, j + d, r)
                            if r == ROWS - 1:
                                split_max(x + d, (j + d) % 2)
                        if s == NORM_AT and not (first and j == 0):
                            scale_out(x - 1)

            def body(it):
                has_mask = dve.value_load(flags[0:1, bass.ds(it, 1)], min_val=0, max_val=1)
                with dve.If(has_mask != 0):
                    wait(dve, mk_ready, 2 * ST * (it + 1))
                    halves(it, True)
                with dve.Else():
                    wait(dve, k_masked, 4 * EXPS * it)
                    dve.sem_inc(k_masked, 4 * EXPS)
                    halves(it, False)
            fours(dve, body)
            add_pair(NX - 1, 0)
            add_pair(NX - 1, 1)
            invert(NX - 1)
            scale_out(NX - 1)



def project_out(nc, x, wo, bo, gamma, beta, scratch, out):
    o_v = scratch["o"].rearrange("i g p l -> i p g l")
    x_v = x.rearrange("b (n t p) c -> (b n) p t c", t=TT, p=P)
    out_v = out.rearrange("b (n t p) c -> (b n) t p c", t=TT, p=P)
    wo_v = wo.rearrange("(k p) n -> p k n", p=P)
    STATS = nc.vector.BN_STATS_DIM
    NC = H // CH

    with ExitStack() as st:
        sb = lambda name, shape, dt: st.enter_context(nc.sbuf_tensor(name, shape, dt))
        sem = lambda name: st.enter_context(nc.semaphore(name))
        o_in = sb("o_in", [P, CT, CH], F32)
        oT_hi = [sb(f"oT_hi{i}", [P, CT, CH], F32R) for i in range(2)]
        oT_lo = [sb(f"oT_lo{i}", [P, CT, CH], F32R) for i in range(2)]
        x_res = [sb(f"x_res{i}", [P, TT, H], F32) for i in range(2)]
        wo_hi, wo_lo = sb("wo_hi", [P, CT, H], F32R), sb("wo_lo", [P, CT, H], F32R)
        bo_r = sb("bo_r", [P, H], F32)
        gamma_r, beta_r = sb("gamma_r", [P, H], F32), sb("beta_r", [P, H], F32)
        y, z = sb("y", [P, 2, H], F32), sb("z", [P, 2, H], F32)
        stats, mv = sb("stats", [P, NC, STATS], F32), sb("mv", [P, 2, 2], F32)
        std, rstd, shift = sb("std", [P, 2], F32), sb("rstd", [P, 2], F32), sb("shift", [P, 2], F32)
        eps = sb("eps", [P, 1], F32)
        acc = [st.enter_context(nc.psum_tensor(f"acc{i}", [P, H], F32)) for i in range(TT)]
        w_raw = [x_res[i][:].rearrange("p t (h c) -> p (t h) c", c=CH) for i in range(NC)]

        w_loaded = [sem(f"wo_loaded{i}") for i in range(CT // 2)]
        w2_loaded = sem("wo2_loaded")
        o_first = [sem(f"o_first{i}") for i in range(CT // 2)]
        o_loaded, bo_loaded, affine_loaded = sem("o_loaded"), sem("bo_loaded"), sem("affine_loaded")
        x_loaded = [sem(f"xr_loaded{i}") for i in range(2)]
        w_hi, w_lo, x_biased, consts_set = sem("wo_hi_done"), sem("wo_lo_done"), sem("x_biased"), sem("consts3_set")
        o_hi, o_lo = sem("o_hi"), sem("o_lo")
        projected, summed, measured, rooted = sem("projected"), sem("summed"), sem("measured"), sem("rooted")
        inverted, centred, scaled, done = sem("inverted"), sem("centred"), sem("scaled"), sem("done")
        statted, weighed, seen = sem("statted"), sem("weighed"), sem("seen3")
        stored = [sem(f"stored{i}") for i in range(2)]
        Q, QK = 4, CT // 4

        def pieces(c, t):
            if isinstance(c, int) and c == 0:
                return range(Q) if t == 0 else ()
            return () if isinstance(c, int) and c == NCH - 1 else ((), (0,), (1,), (2, 3))[t]

        block = st.enter_context(nc.Block())

        @block.sync
        def _(sp):
            def load_o(c):
                sp.dma_start(o_in[:], o_v[bass.ds(c, 1)].rearrange("o p g l -> (o p) g l")).then_inc(o_loaded, 16)

            def load_x(c, r):
                sp.dma_start(x_res[r][:], x_v[bass.ds(c, 1)].rearrange("o p t c -> (o p) t c")).then_inc(x_loaded[r], 16)

            for i in range(Q):
                two = slice(QK * i, QK * (i + 1))
                sp.dma_start(w_raw[0][:, two], wo_v[:, two, 0:CH]).then_inc(w_loaded[i], 16)
                sp.dma_start(o_in[:, two], o_v[0, :, two]).then_inc(o_first[i], 16)
            sp.dma_start(w_raw[1], wo_v[:, :, CH:H]).then_inc(w2_loaded, 16)
            sp.dma_start(bo_r[:], bo.partition_broadcast(P)).then_inc(bo_loaded, 16)
            sp.dma_start(gamma_r[:], gamma.partition_broadcast(P)).then_inc(affine_loaded, 16)
            sp.dma_start(beta_r[:], beta.partition_broadcast(P)).then_inc(affine_loaded, 16)
            sp.wait_ge(o_lo, Q)
            load_o(1)
            for i in range(2):
                sp.wait_ge(w_lo, CT * (i + 1))
                load_x(i, i)

            def body(it, last):
                for r in range(2):
                    c = 2 * it + r
                    for t in range(TT):
                        k = TT * c + t
                        if t == TT - 2 and not last:
                            wait(sp, o_lo, Q * (c + 2))
                            load_o(c + 2)
                        wait(sp, done, k + 1)
                        sp.dma_start(out_v[bass.ds(c, 1), t].rearrange("o p c -> (o p) c"), z[:, t % 2]).then_inc(stored[t % 2], 16)
                    if not last:
                        wait(sp, summed, TT * (c + 1))
                        load_x(c + 2, r)
            with sp.Fori(0, NCH // 2 - 1) as it:
                body(it, False)
            body(NCH // 2 - 1, True)
            for r in range(2):
                sp.wait_ge(stored[r], 16 * NCH * TT // 2)

        @block.tensor
        def _(pe):
            def terms(bank, r, g, t, cols):
                tok = slice(t * P, (t + 1) * P)
                for n, (a, w) in enumerate(((oT_hi[r], wo_hi), (oT_hi[r], wo_lo), (oT_lo[r], wo_hi))):
                    last = nc.tensor.matmul(bank, a[:, g, tok], w[:, g, cols], start=g == 0 and n == 0, stop=g == CT - 1 and n == 2)
                return last

            cols = slice(0, CH)
            for g in range(CT):
                pe.wait_ge(w_lo, g + 1)
                pe.wait_ge(o_lo, g // QK + 1)
                for t in range(TT):
                    terms(acc[t][:, cols], 0, g, t, cols)
            pe.wait_ge(w_lo, NC * CT)
            for t in range(TT):
                for g in range(CT):
                    last = terms(acc[t][:, CH:H], 0, g, t, slice(CH, H))
                last.then_inc(projected, 1)

            def chunk(c, r):
                for t in range(TT):
                    if t == 0:
                        wait(pe, o_lo, Q * (c + 1))
                    wait(pe, summed, TT * (c - 1) + t + 1)
                    for n in range(NC):
                        cols = slice(n * CH, (n + 1) * CH)
                        for g in range(CT):
                            last = terms(acc[t][:, cols], r, g, t, cols)
                    last.then_inc(projected, 1)
            chunk(1, 1)
            with pe.Fori(1, NCH // 2) as it:
                for r in range(2):
                    chunk(2 * it + r, r)

        @block.scalar
        def _(act):
            def split_wo(n, k):
                act.wait_ge(w2_loaded if n else w_loaded[k // 2], 16)
                nc.scalar.activation(wo_hi[:, k, n * CH:(n + 1) * CH], w_raw[n][:, k], ACT.Copy).then_inc(w_hi, 1)

            def split_hi(c, r, j):
                nc.scalar.activation(oT_hi[r][:, QK * j:QK * (j + 1)].rearrange("p g l -> p (g l)"),
                                     o_in[:, QK * j:QK * (j + 1)].rearrange("p g l -> p (g l)"), ACT.Copy).then_inc(o_hi, 1)

            for j in range(Q):
                for k in range(QK):
                    split_wo(0, QK * j + k)
                act.wait_ge(o_first[j], 16)
                split_hi(0, 0, j)
            for k in range(CT):
                split_wo(1, k)
            act.wait_ge(consts_set, 1)

            def body(it, last):
                for r in range(2):
                    c = 2 * it + r
                    for t in range(TT):
                        k = TT * c + t
                        for j in pieces(c, t):
                            if j == 0:
                                wait(act, o_loaded, 16 * (c + 1))
                                wait(act, projected, TT * c)
                            split_hi(c + 1, 1 - r, j)
                        wait(act, measured, k + 1)
                        nc.scalar.activation(std[:, t % 2:t % 2 + 1], mv[:, t % 2, 1:2], ACT.Sqrt, bias=eps[:]).then_inc(rooted, 1)
                        wait(act, centred, k + 1)
                        wait(act, stored[t % 2], 16 * (TT // 2 * c + t // 2))
                        nc.scalar.activation(z[:, t % 2], y[:, t % 2], ACT.Identity, scale=rstd[:, t % 2:t % 2 + 1],
                                             bias=shift[:, t % 2:t % 2 + 1]).then_inc(scaled, 1)
            body(0, False)
            with act.Fori(1, NCH // 2 - 1) as it:
                body(it, False)
            body(NCH // 2 - 1, True)

        @block.gpsimd
        def _(pool):
            pool.wait_ge(bo_loaded, 16)

            def body(it):
                for r in range(2):
                    c = 2 * it + r
                    wait(pool, x_loaded[r], 16 * (it + 1))
                    for t in range(TT):
                        nc.gpsimd.tensor_tensor(x_res[r][:, t], x_res[r][:, t], bo_r[:], ALU.add).then_inc(x_biased, 1)
            body(0)
            with pool.Fori(1, NCH // 2) as it:
                body(it)

        @block.vector
        def _(dve):
            nc.vector.memset(eps[:], EPS).then_inc(consts_set, 1)

            def split_wo(n, k):
                cols = slice(n * CH, (n + 1) * CH)
                dve.wait_ge(w_hi, CT * n + k + 1)
                nc.vector.tensor_tensor(wo_lo[:, k, cols], w_raw[n][:, k], f32(wo_hi[:, k, cols]), ALU.subtract).then_inc(w_lo, 1)

            def split_lo(c, r, j):
                flat = lambda a: a[:, QK * j:QK * (j + 1)].rearrange("p g l -> p (g l)")
                wait(dve, o_hi, Q * c + j + 1)
                nc.vector.tensor_tensor(flat(oT_lo[r]), flat(o_in), f32(flat(oT_hi[r])), ALU.subtract).then_inc(o_lo, 1)

            for j in range(Q):
                for k in range(QK):
                    split_wo(0, QK * j + k)
                split_lo(0, 0, j)
            for k in range(CT):
                split_wo(1, k)
            dve.wait_ge(affine_loaded, 32)

            def measure(c, r, t):
                k, s = TT * c + t, t % 2
                wait(dve, x_biased, k + 1)
                wait(dve, projected, k + 1)
                nc.vector.tensor_tensor(y[:, s], acc[t][:], x_res[r][:, t], ALU.add).then_inc(summed, 1)
                wait(dve, summed, k + 1)
                for n in range(NC):
                    nc.vector.bn_stats(stats[:, n], y[:, s, n * CH:(n + 1) * CH]).then_inc(statted, 1)
                wait_before(dve, statted, NC * (k + 1), seen)
                nc.vector.bn_aggr(mv[:, s], stats[:].rearrange("p n s -> p (n s)")).then_inc(measured, 1)

            def centre(c, r, t):
                k, s = TT * c + t, t % 2
                wait(dve, rooted, k + 1)
                nc.vector.reciprocal(rstd[:, s:s + 1], std[:, s:s + 1]).then_inc(inverted, 1)
                wait(dve, inverted, k + 1)
                nc.vector.tensor_scalar(shift[:, s:s + 1], mv[:, s, 0:1], rstd[:, s:s + 1], -1.0, ALU.mult, ALU.mult).then_inc(centred, 1)

            def weigh(c, r, t):
                k, s = TT * c + t, t % 2
                wait(dve, scaled, k + 1)
                nc.vector.tensor_tensor(z[:, s], z[:, s], gamma_r[:], ALU.mult).then_inc(weighed, 1)
                wait(dve, weighed, k + 1)
                nc.vector.tensor_tensor(z[:, s], z[:, s], beta_r[:], ALU.add).then_inc(done, 1)

            def body(it):
                for r in range(2):
                    c = 2 * it + r
                    for t in range(TT):
                        for j in pieces(c, t):
                            split_lo(c + 1, 1 - r, j)
                        measure(c, r, t)
                        if t > 0:
                            weigh(c, r, t - 1)
                        elif not (isinstance(c, int) and c == 0):
                            weigh(c - 1, 1 - r, TT - 1)
                        centre(c, r, t)
            body(0)
            with dve.Fori(1, NCH // 2 - 1) as it:
                body(it)
            body(NCH // 2 - 1)
            weigh(NCH - 1, 1, TT - 1)



_INS = ["x", "ctx_2048", "mask_Bx1xSxS2_ff0", "L0_xattn_Wq", "L0_xattn_bq", "L0_xattn_Wk", "L0_xattn_bk", "L0_xattn_Wv",
        "L0_xattn_bv", "L0_xattn_Wo", "L0_xattn_bo", "L0_xattn_gamma", "L0_xattn_beta"]


def cross_attention(nc, x, context, mask, wq, bq, wk, bk, wv, bv, wo, bo, gamma, beta, ident, out):
    dram = lambda name, shape: nc.dram_tensor(name, shape, F32, kind="Internal").ap()
    scratch = {"q_hi": dram("q_hi_s", [NCH, KVH, P, CH]), "q_lo": dram("q_lo_s", [NCH, KVH, P, CH]),
               "k_hi": dram("k_hi_s", [NCH, E, CH]), "k_lo": dram("k_lo_s", [NCH, E, CH]),
               "v": dram("v_s", [B * L, E]), "o": dram("o_s", [NCH, KVH, P, CH])}
    with nc.sbuf_tensor("flags", [P, PAIRS], I32) as flags:
        project_qkv(nc, x, context, mask, wq, bq, wk, bk, wv, bv, ident, scratch, flags)
        attend(nc, mask, ident, scratch, flags)
    project_out(nc, x, wo, bo, gamma, beta, scratch, out)


def kernel(**inputs):
    import numpy as _np
    import concourse.bacc as _bacc
    from concourse.bass_utils import run_bass_kernel_spmd as _run

    nc = _bacc.Bacc("TRN2", target_bir_lowering=False, num_devices=1, dynamic_dma_scratch_size=1024)
    arrays = {f"in_{name}": _np.ascontiguousarray(inputs[name]) for name in _INS}
    arrays["in_identity"] = _np.eye(P, dtype=_np.float32)
    args = [nc.dram_tensor(name, a.shape, mybir.dt.from_np(a.dtype), kind="ExternalInput").ap() for name, a in arrays.items()]
    out = nc.dram_tensor("out_0", (B, L, H), F32, kind="ExternalOutput").ap()
    cross_attention(nc, *args, out)
    result = _run(nc, [arrays], core_ids=[0])
    return result.results[0]["out_0"]
```
